# Optimizing a Trainium2 kernel written in Bass

```python
import numpy as np
import jax
import jax.numpy as jnp

def _softmax(x, axis=-1):
    return jax.nn.softmax(x, axis=axis)

def _gelu(x):
    return jax.nn.gelu(x, approximate=True)

def _silu(x):
    return jax.nn.silu(x)

def _sigmoid(x):
    return jax.nn.sigmoid(x)

def _layernorm(x, axis=-1, eps=1e-05):
    m = jnp.mean(x, axis=axis, keepdims=True)
    v = jnp.var(x, axis=axis, keepdims=True)
    return (x - m) / jnp.sqrt(v + eps)

def _scatter_add(tgt, idx, src, axis=0):
    return tgt.at[idx].add(src)

def _segment_sum(src, seg, n):
    return jax.ops.segment_sum(src, seg, n)
kernel_name = 'mk_prb_d1_jaxref_r4_b4ee80'

def setup_inputs(seed: int=0):
    np.random.seed(seed)
    _w = jnp.asarray

    def _L0_attn_setup():
        import jax, jax.numpy as jnp
        import numpy as np
        HEADS = 16
        LOCAL_HEADS = 4
        DIM = 256
        DH = DIM // HEADS
        WINDOW = 128
        BLINDSPOT = 64

        def _look_around(x, buckets):
            pad_cfg = ((0, 0), (1, 0)) + ((0, 0),) * (x.ndim - 2)
            pv = -1.0 if jnp.issubdtype(x.dtype, jnp.floating) else -1
            p = jnp.pad(x, pad_cfg, constant_values=pv)
            return jnp.concatenate([p[:, :buckets], p[:, 1:buckets + 1]], axis=2)

        def _local_attn(q, k, v):
            b, lh, t, e = q.shape
            bm = b * lh
            buckets = t // WINDOW
            bq = q.reshape(bm, buckets, WINDOW, e)
            bk = k.reshape(bm, buckets, WINDOW, e)
            bv = v.reshape(bm, buckets, WINDOW, e)
            bk2 = _look_around(bk, buckets)
            bv2 = _look_around(bv, buckets)
            ticker = jnp.arange(t, dtype=jnp.int32).reshape(1, buckets, WINDOW)
            bq_k = _look_around(ticker, buckets)
            dots = jnp.einsum('buie,buje->buij', bq, bk2) * e ** (-0.5)
            mask_value = -jnp.finfo(dots.dtype).max
            causal_mask = ticker[:, :, :, None] < bq_k[:, :, None, :]
            pad_mask = bq_k[:, :, None, :] == -1
            dots = jnp.where(causal_mask | pad_mask, mask_value, dots)
            attn = jax.nn.softmax(dots, axis=-1)
            out = jnp.einsum('buij,buje->buie', attn, bv2)
            return out.reshape(b, lh, t, e)

        def _causal_linear_attn(q, k, v):
            b, h, n, e = q.shape
            u = n // BLINDSPOT
            q = jax.nn.softmax(q, axis=-1)
            k = jax.nn.elu(k) + 1.0
            bq = q.reshape(b, h, u, BLINDSPOT, e)
            bk = k.reshape(b, h, u, BLINDSPOT, e)
            bv = v.reshape(b, h, u, BLINDSPOT, e)
            bk_cumsum = jnp.cumsum(bk.sum(axis=-2), axis=-2)
            ctx = jnp.einsum('bhund,bhune->bhude', bk, bv)
            ctx = jnp.cumsum(ctx, axis=2)
            ctx = ctx / (bk_cumsum[..., None] + 1e-06)
            ctx = jnp.pad(ctx, ((0, 0), (0, 0), (1, 0), (0, 0), (0, 0)))[:, :, :u]
            attn = jnp.einsum('bhund,bhude->bhune', bq, ctx)
            return attn.reshape(b, h, n, e)
        key = jax.random.key(seed)
        ks = jax.random.split(key, 6)
        s = 1.0 / np.sqrt(DIM)
        x = jax.random.normal(ks[0], (4, 2048, DIM), dtype=jnp.float32)
        Wq = jax.random.normal(ks[1], (DIM, DIM), dtype=jnp.float32) * s
        Wk = jax.random.normal(ks[2], (DIM, DIM), dtype=jnp.float32) * s
        Wv = jax.random.normal(ks[3], (DIM, DIM), dtype=jnp.float32) * s
        Wo = jax.random.normal(ks[4], (DIM, DIM), dtype=jnp.float32) * s
        bo = jax.random.normal(ks[5], (DIM,), dtype=jnp.float32) * 0.01
        return {'x': x, 'Wq': Wq, 'Wk': Wk, 'Wv': Wv, 'Wo': Wo, 'bo': bo}
    _L0_attn_in = _L0_attn_setup()

    def _L0_ffn_setup():
        import jax, jax.numpy as jnp
        import numpy as np
        HIDDEN = 256
        NUM_EXPERTS = 8
        TOP_K = 2
        FFN = 1024
        BATCH, SEQ = (4, 512)
        key = jax.random.key(seed)
        k_x, k_r, k_w1, k_w2 = jax.random.split(key, 4)
        x = jax.random.normal(k_x, (BATCH, SEQ, HIDDEN), dtype=jnp.float32)
        router_w = jax.random.normal(k_r, (NUM_EXPERTS, HIDDEN), dtype=jnp.float32) * (1.0 / np.sqrt(HIDDEN))
        lim = float(np.sqrt(6.0 / (FFN + HIDDEN)))
        expert_w1 = jax.random.uniform(k_w1, (NUM_EXPERTS, FFN, HIDDEN), dtype=jnp.float32, minval=-lim, maxval=lim)
        expert_w2 = jax.random.uniform(k_w2, (NUM_EXPERTS, HIDDEN, FFN), dtype=jnp.float32, minval=-lim, maxval=lim)
        return {'x': x, 'router_w': router_w, 'expert_w1': expert_w1, 'expert_w2': expert_w2}
    _L0_ffn_in = _L0_ffn_setup()
    _d = {'L0_attn_x': _L0_attn_in['x'], 'L0_attn_Wq': _L0_attn_in['Wq'], 'L0_attn_Wk': _L0_attn_in['Wk'], 'L0_attn_Wv': _L0_attn_in['Wv'], 'L0_attn_Wo': _L0_attn_in['Wo'], 'L0_attn_bo': _L0_attn_in['bo'], 'L0_ffn_router_w': _L0_ffn_in['router_w'], 'L0_ffn_expert_w1': _L0_ffn_in['expert_w1'], 'L0_ffn_expert_w2': _L0_ffn_in['expert_w2']}
    _x0 = _d['L0_attn_x']
    _d['L0_attn_x'] = jax.random.normal(jax.random.fold_in(jax.random.key(seed), 1), (2, 2048, 256), dtype=_x0.dtype)
    del _x0
    return _d

def reference(L0_attn_x, L0_attn_Wq, L0_attn_Wk, L0_attn_Wv, L0_attn_Wo, L0_attn_bo, L0_ffn_router_w, L0_ffn_expert_w1, L0_ffn_expert_w2):

    def _L0_attn_ref(x, Wq, Wk, Wv, Wo, bo):
        import jax, jax.numpy as jnp
        import numpy as np
        HEADS = 16
        LOCAL_HEADS = 4
        DIM = 256
        DH = DIM // HEADS
        WINDOW = 128
        BLINDSPOT = 64

        def _look_around(x, buckets):
            pad_cfg = ((0, 0), (1, 0)) + ((0, 0),) * (x.ndim - 2)
            pv = -1.0 if jnp.issubdtype(x.dtype, jnp.floating) else -1
            p = jnp.pad(x, pad_cfg, constant_values=pv)
            return jnp.concatenate([p[:, :buckets], p[:, 1:buckets + 1]], axis=2)

        def _local_attn(q, k, v):
            b, lh, t, e = q.shape
            bm = b * lh
            buckets = t // WINDOW
            bq = q.reshape(bm, buckets, WINDOW, e)
            bk = k.reshape(bm, buckets, WINDOW, e)
            bv = v.reshape(bm, buckets, WINDOW, e)
            bk2 = _look_around(bk, buckets)
            bv2 = _look_around(bv, buckets)
            ticker = jnp.arange(t, dtype=jnp.int32).reshape(1, buckets, WINDOW)
            bq_k = _look_around(ticker, buckets)
            dots = jnp.einsum('buie,buje->buij', bq, bk2) * e ** (-0.5)
            mask_value = -jnp.finfo(dots.dtype).max
            causal_mask = ticker[:, :, :, None] < bq_k[:, :, None, :]
            pad_mask = bq_k[:, :, None, :] == -1
            dots = jnp.where(causal_mask | pad_mask, mask_value, dots)
            attn = jax.nn.softmax(dots, axis=-1)
            out = jnp.einsum('buij,buje->buie', attn, bv2)
            return out.reshape(b, lh, t, e)

        def _causal_linear_attn(q, k, v):
            b, h, n, e = q.shape
            u = n // BLINDSPOT
            q = jax.nn.softmax(q, axis=-1)
            k = jax.nn.elu(k) + 1.0
            bq = q.reshape(b, h, u, BLINDSPOT, e)
            bk = k.reshape(b, h, u, BLINDSPOT, e)
            bv = v.reshape(b, h, u, BLINDSPOT, e)
            bk_cumsum = jnp.cumsum(bk.sum(axis=-2), axis=-2)
            ctx = jnp.einsum('bhund,bhune->bhude', bk, bv)
            ctx = jnp.cumsum(ctx, axis=2)
            ctx = ctx / (bk_cumsum[..., None] + 1e-06)
            ctx = jnp.pad(ctx, ((0, 0), (0, 0), (1, 0), (0, 0), (0, 0)))[:, :, :u]
            attn = jnp.einsum('bhund,bhude->bhune', bq, ctx)
            return attn.reshape(b, h, n, e)
        b, t, dim = x.shape
        q = x @ Wq
        k = x @ Wk
        v = x @ Wv
        mh = lambda z: z.reshape(b, t, HEADS, DH).transpose(0, 2, 1, 3)
        q, k, v = (mh(q), mh(k), mh(v))
        lq, gq = (q[:, :LOCAL_HEADS], q[:, LOCAL_HEADS:])
        lk, gk = (k[:, :LOCAL_HEADS], k[:, LOCAL_HEADS:])
        lv, gv = (v[:, :LOCAL_HEADS], v[:, LOCAL_HEADS:])
        local_out = _local_attn(lq, lk, lv)
        global_out = _causal_linear_attn(gq, gk, gv)
        attn = jnp.concatenate([local_out, global_out], axis=1)
        attn = attn.transpose(0, 2, 1, 3).reshape(b, t, dim)
        return attn @ Wo + bo

    def _L0_ffn_ref(x, router_w, expert_w1, expert_w2):
        import jax, jax.numpy as jnp
        import numpy as np
        HIDDEN = 256
        NUM_EXPERTS = 8
        TOP_K = 2
        FFN = 1024
        BATCH, SEQ = (4, 512)
        B, S, D = x.shape
        xf = x.reshape(-1, D)
        scores = xf @ router_w.T
        top_v, top_i = jax.lax.top_k(scores, TOP_K)
        routing_w = jax.nn.softmax(top_v, axis=-1)
        out = jnp.zeros_like(xf)
        for e in range(NUM_EXPERTS):
            w_e = jnp.sum(jnp.where(top_i == e, routing_w, 0.0), axis=-1)
            h = jax.nn.gelu(xf @ expert_w1[e].T, approximate=False)
            out = out + h @ expert_w2[e].T * w_e[:, None]
        return out.reshape(B, S, D)
    x = L0_attn_x
    xn = _layernorm(x, axis=-1)
    x = x + _L0_attn_ref(xn, L0_attn_Wq, L0_attn_Wk, L0_attn_Wv, L0_attn_Wo, L0_attn_bo) + _L0_ffn_ref(xn, L0_ffn_router_w, L0_ffn_expert_w1, L0_ffn_expert_w2)
    return x

_drawn_inputs = setup_inputs


def setup_inputs(seed=0):
    import zlib

    import numpy as np

    out = dict(_drawn_inputs(seed))
    spreads = {}
    factors = {'L0_attn_bo': 5.766}
    for name, (base, spread) in spreads.items():
        noise = np.random.default_rng([zlib.crc32(name.encode()), seed]).standard_normal(out[name].shape)
        drawn = base * np.exp(spread * noise) if base else spread * noise
        out[name] = jnp.asarray(drawn.astype(out[name].dtype))
    for name, factor in factors.items():
        out[name] = (out[name] * factor).astype(out[name].dtype)
    return out
```

```python
from contextlib import ExitStack

import concourse.bass as bass
from concourse import mybir

ALU = mybir.AluOpType
ACT = mybir.ActivationFunctionType
F32 = mybir.dt.float32
F16 = mybir.dt.float16
I32 = mybir.dt.int32
AX = mybir.AxisListType.X

P = 128
B, SEQ, D = 2, 2048, 256
TOK = B * SEQ
NT = TOK // P
NW = SEQ // P
HEADS, LH, DH = 16, 4, 16
GD = (HEADS - LH) * DH
LD = LH * DH
KC = D // P
E, F, TOPK = 8, 1024, 2
FC = F // P
NB = (TOK * TOPK) // P + E
PAD = P
BIG = 3.0e38
XS, WS, HS, AS = 256.0, 64.0, 16.0, 64.0
UN_XW, UN_AW, UN_HW = 1 / (XS * WS), 1 / (AS * WS), 1 / (HS * WS)
CQ, CK, CR, CV = 0, GD, 2 * GD, 2 * GD + E
NTOKC = CV + D
GA, GB = 128, 64
CTX = GA + 1 + GB + 1
VC = LD + CTX
DS = bass.ds


def block_kernel(nc, x, wq, wk, wv, wo, bo, rwt, w1c, w2c, out):
    with ExitStack() as ctx:
        def sb(name, shape, dt=F32):
            return ctx.enter_context(nc.sbuf_tensor(name, shape, dt))

        def sem(name):
            return ctx.enter_context(nc.semaphore(name))

        def pair(name, shape, dt=F32):
            return [sb(f"{name}{b}", shape, dt) for b in range(2)]

        xn_rows = nc.dram_tensor("xn_rows", (TOK + PAD, D), F32).ap()

        w1h, w1l = sb("w1h", [P, E * KC * F], F16), sb("w1l", [P, E * KC * F], F16)
        w2h, w2l = sb("w2h", [P, E * FC * D], F16), sb("w2l", [P, E * FC * D], F16)
        stage = pair("stage", [P, F])
        wtok = [sb(f"wtok{n}", [P, KC, NTOKC], F16) for n in "hl"]
        wqk = [sb(f"wqk{n}", [P, KC, 2, LH, 32], F16) for n in "hl"]
        wout = [sb(f"wout{n}", [P, KC, D], F16) for n in "hl"]
        ident = sb("ident", [P, P])
        causal = sb("causal", [P, 2 * P])
        ctx_mask = sb("ctx_mask", [P, CTX])
        bias = sb("bias", [P, D])
        minus_half = sb("minus_half", [P, 1])
        scores = sb("scores", [P, NT, E])

        xin, xn, xb = pair("xin", [P, D]), pair("xn", [P, D]), pair("xb", [P, D])
        stats, mv = pair("stats", [P, 6]), pair("mv", [P, 2])
        veps, rstd = pair("veps", [P, 1]), pair("rstd", [P, 1])
        xth, xtl = pair("xth", [P, D], F16), pair("xtl", [P, D], F16)
        qt, kt = pair("qt", [P, P]), pair("kt", [P, 2 * P])
        val, vprev = pair("val", [P, VC]), pair("vprev", [P, LD])
        qmax, qsum, qrec = pair("qmax", [P, 12]), pair("qsum", [P, 12]), pair("qrec", [P, 12])
        qs, krelu, ke = pair("qs", [P, D]), pair("krelu", [P, GD]), pair("ke", [P, D])
        ss, pt = pair("ss", [P, LH, 2 * P]), pair("pt", [P, LH, 2, P])
        negmax, rsum, rrec = pair("negmax", [P, LH]), pair("rsum", [P, LH]), pair("rrec", [P, LH])
        cum, cum0 = pair("cum", [P, CTX]), pair("cum0", [P, CTX])
        new0, new1 = pair("new0", [P, CTX]), pair("new1", [P, CTX])
        den, rden = pair("den", [P, 2, 2]), pair("rden", [P, 2, 2])
        qgt = pair("qgt", [P, 2, P])
        attn, res = pair("attn", [P, D]), pair("res", [P, D])
        rows_from, rows_to = pair("rows_from", [P, 1], I32), pair("rows_to", [P, 1], I32)
        ath, atl = pair("ath", [P, D], F16), pair("atl", [P, D], F16)

        bank = [ctx.enter_context(nc.psum_tensor(f"bank{n}", [P, 512], F32)) for n in range(8)]
        bA, bB, bC, bD = ([bank[4 * b + n] for b in range(2)] for n in range(4))

        got_w, got_c = sem("got_w"), sem("got_c")
        pool_const, zeroed, padded = sem("pool_const"), sem("zeroed"), sem("padded")
        w_hi, w_lo = sem("w_hi"), sem("w_lo")

        names = ("stats_in aggregated veps_in rstd_in xn_in xb_in xnt xth_in xtl_in tok0 tok1 qt_in kt_in "
                 "v_in qmax_in qsub_in qexp_in kexp_in tok0_read qsum_in qrec_in qn_in ke_in qgt_ps "
                 "head0 head2 s_ps negmax_in mask_open prob pt_ps pta_in ptb_in ctx_ps new_in cum0_in "
                 "den_in rden_in qgt_in att_ps rrec_in attn_in cum_in at_ps ath_in atl_in pr_ps res_in "
                 "prev_kept stage_up stage_hi stage_lo").split()
        s = {n: sem(n) for n in names}
        x_loaded = [sem(f"x_loaded{b}") for b in range(2)]
        xn_stored = [sem(f"xn_stored{b}") for b in range(2)]
        res_stored = [sem(f"res_stored{b}") for b in range(2)]
        w_loaded = [sem(f"w_loaded{b}") for b in range(2)]

        wsrc = {"q": ss[0][:, 0:2, :], "k": ss[0][:, 2:4, :], "v": ss[1][:, 0:2, :], "o": ss[1][:, 2:4, :]}
        rsrc = qs[0][:, 0:KC * E].rearrange("p (k e) -> p k e", k=KC)

        with nc.Block() as block:
            @block.sync
            def _(sp):
                for name, w in (("q", wq), ("k", wk), ("v", wv), ("o", wo)):
                    sp.dma_start(wsrc[name], w.rearrange("(k p) n -> p k n", p=P)).then_inc(got_w, 16)
                sp.dma_start(rsrc, rwt.rearrange("(k p) n -> p k n", p=P)).then_inc(got_w, 16)
                sp.dma_start(bias[:], bo.partition_broadcast(P)).then_inc(got_c, 16)
                sp.wait_ge(zeroed, 1)
                sp.dma_start(xn_rows[TOK:TOK + PAD, :], xn[0][:]).then_inc(padded, 16)
                sp.dma_start(out[TOK:TOK + PAD, :], xn[0][:]).then_inc(padded, 16)
                sp.wait_ge(got_c, 16)
                sp.wait_ge(padded, 32)
                for b in range(2):
                    sp.sem_inc(xn_stored[b], 16)
                    sp.sem_inc(res_stored[b], 16)

            @block.gpsimd
            def _(pool):
                pool.memset(ident[:], 0.0).then_inc(pool_const, 1)
                pool.memset(causal[:, 0:P], BIG).then_inc(pool_const, 1)
                pool.memset(causal[:, P:2 * P], 0.0).then_inc(pool_const, 1)
                pool.memset(ctx_mask[:], 1.0).then_inc(pool_const, 1)
                pool.memset(minus_half[:], -0.5).then_inc(pool_const, 1)
                pool.wait_ge(pool_const, 5)
                pool.affine_select(out=ident[:], in_=ident[:], compare_op=ALU.not_equal, fill=1.0, base=0,
                                   pattern=[[-1, P]], channel_multiplier=1).then_inc(pool_const, 1)
                pool.affine_select(out=causal[:, P:2 * P], in_=causal[:, P:2 * P], compare_op=ALU.is_ge,
                                   fill=BIG, base=0, pattern=[[-1, P]], channel_multiplier=1).then_inc(pool_const, 1)
                step = 7
                for c0, width in ((0, GA), (GA + 1, GB)):
                    v = ctx_mask[:, c0:c0 + width].rearrange("p (h e) -> p h e", e=DH)
                    for base, mult, sign in ((0, 1, -DH), (DH - 1, -1, DH)):
                        pool.wait_ge(pool_const, step)
                        pool.affine_select(out=v, in_=v, compare_op=ALU.is_ge, fill=0.0, base=base,
                                           pattern=[[sign, width // DH], [0, DH]],
                                           channel_multiplier=mult).then_inc(pool_const, 1)
                        step += 1
                for n in ("rstd_in", "xb_in", "ke_in", "prev_kept", "stage_up", "stage_lo"):
                    pool.sem_inc(s[n], 2)

            @block.scalar
            def _(act):
                for n in ("xth_in", "qt_in", "kt_in", "v_in", "qexp_in", "kexp_in", "tok0_read",
                          "prob", "ptb_in", "ath_in", "stage_hi"):
                    act.sem_inc(s[n], 2)

            @block.tensor
            def _(pe):
                for n in ("xnt", "tok0", "tok1", "qgt_ps", "head0", "head2", "s_ps", "pt_ps", "ctx_ps",
                          "att_ps", "at_ps", "pr_ps"):
                    pe.sem_inc(s[n], 2)

            @block.vector
            def _(dve):
                dve.memset(xn[0][:], 0.0).then_inc(zeroed, 1)
                for b in range(2):
                    dve.memset(kt[b][:], 0.0)
                    dve.memset(vprev[b][:], 0.0)
                    dve.memset(cum[b][:], 0.0)
                    dve.memset(ke[b][:, GD:D], 0.0)
                    dve.memset(val[b][:, LD + GA:LD + GA + 1], 1.0)
                    dve.memset(val[b][:, VC - 1:VC], 1.0)
                for n in range(2):
                    dve.memset(wqk[n][:], 0.0).then_inc(zeroed, 1)
                dve.wait_ge(got_w, 80)
                dve.wait_ge(zeroed, 3)
                jobs = [(lambda n: wtok[n][:, :, CQ:CQ + GD], wsrc["q"][:, :, LD:D]),
                        (lambda n: wtok[n][:, :, CK:CK + GD], wsrc["k"][:, :, LD:D]),
                        (lambda n: wtok[n][:, :, CR:CR + E], rsrc),
                        (lambda n: wtok[n][:, :, CV:CV + D], wsrc["v"]),
                        (lambda n: wout[n][:], wsrc["o"])]
                for k in range(KC):
                    for m, name in enumerate("qk"):
                        jobs.append((lambda n, k=k, m=m: wqk[n][:, k, m, :, 0:DH],
                                     wsrc[name][:, k, 0:LD].rearrange("p (h e) -> p h e", e=DH)))
                for dst, src in jobs:
                    dve.tensor_scalar(dst(0), src, WS, None, ALU.mult).then_inc(w_hi, 1)
                for c, (dst, src) in enumerate(jobs):
                    dve.wait_ge(w_hi, c + 1)
                    dve.scalar_tensor_tensor(out=dst(1), in0=src, scalar=WS, in1=dst(0),
                                             op0=ALU.mult, op1=ALU.subtract).then_inc(w_lo, 1)
                dve.wait_ge(w_lo, len(jobs))
                for b in range(2):
                    dve.memset(qs[b][:, GD:D], 0.0)
                for n in ("stats_in", "aggregated", "veps_in", "xn_in", "xtl_in", "qmax_in", "qsub_in",
                          "qsum_in", "qrec_in", "qn_in", "negmax_in", "mask_open", "pta_in", "new_in",
                          "cum0_in", "den_in", "rden_in", "qgt_in", "rrec_in", "attn_in", "cum_in",
                          "atl_in", "res_in"):
                    dve.sem_inc(s[n], 2)

        def stepper(eng, name, first):
            value = eng.alloc_register(name)
            eng.reg_mov(value, first)

            def wait(semaphore):
                eng.wait_ge(semaphore, value)
                eng.reg_add(value, value, 1)
            return wait

        def counts(eng, i):
            if isinstance(i, int):
                return [2 * i + 3, 2 * i + 4], [2 * i + 1, 2 * i + 2]
            return ([eng.snap(2 * i + 3), eng.snap(2 * i + 4)], [eng.snap(2 * i + 1), eng.snap(2 * i + 2)])

        def three(pe, dst, lhs, rhs, chunks):
            terms = [(k, a, c) for k in chunks for a, c in ((0, 0), (0, 1), (1, 0))]
            for n, (k, a, c) in enumerate(terms):
                ins = pe.matmul(dst, lhs(a, k), rhs(c, k), start=(n == 0), stop=(n == len(terms) - 1))
            return ins

        with nc.Block() as block:
            @block.sync
            def _(sp):
                def load_x(b, i):
                    sp.dma_start(xin[b][:], x[DS((b * NW + i) * P, P), :]).then_inc(x_loaded[b], 16)

                def load_weights(i):
                    for m, w in enumerate((w1c, w2c)):
                        sp.dma_start(stage[m][:], w[DS(i * P, P), :]).then_inc(w_loaded[m], 16)

                def window(i, last):
                    now, before = counts(sp, i)
                    for b in range(2):
                        sp.wait_ge(s["xn_in"], now[b])
                        sp.dma_start(xn_rows[DS((b * NW + i) * P, P), :], xn[b][:]).then_inc(xn_stored[b], 16)
                        if not last:
                            sp.wait_ge(s["xb_in"], now[b])
                            load_x(b, i + 1)
                    if not last:
                        for m in range(2):
                            sp.wait_ge(s["stage_lo"], now[m])
                        load_weights(i + 1)
                    for b in range(2):
                        sp.wait_ge(s["res_in"], now[b])
                        sp.dma_start(out[DS((b * NW + i) * P, P), :], res[b][:]).then_inc(res_stored[b], 16)

                for b in range(2):
                    load_x(b, 0)
                load_weights(0)
                with sp.Fori(0, NW - 1) as i:
                    window(i, False)
                window(NW - 1, True)
                for b in range(2):
                    sp.wait_ge(xn_stored[b], 16 * (NW + 1))
                    sp.wait_ge(res_stored[b], 16 * (NW + 1))

            @block.gpsimd
            def _(pool):
                wait_hi, wait_att = stepper(pool, "hi_value", 3), stepper(pool, "att_value", 3)
                with pool.Fori(0, NW) as i:
                    now, before = counts(pool, i)
                    for b in range(2):
                        pool.wait_ge(s["veps_in"], now[b])
                        pool.tensor_tensor(rstd[b][:], veps[b][:], minus_half[:], ALU.pow).then_inc(s["rstd_in"], 1)
                    for b in range(2):
                        pool.wait_ge(x_loaded[b], 16 * i + 16)
                        pool.wait_ge(s["res_in"], before[b])
                        pool.tensor_tensor(xb[b][:], xin[b][:], bias[:], ALU.add).then_inc(s["xb_in"], 1)
                    for b in range(2):
                        pool.wait_ge(s["kexp_in"], now[b])
                        pool.tensor_tensor(ke[b][:, 0:GD], ke[b][:, 0:GD], krelu[b][:], ALU.add).then_inc(s["ke_in"], 1)
                    for m, lo in enumerate((w1l, w2l)):
                        wait_hi(s["stage_hi"])
                        pool.tensor_scalar(stage[m][:], stage[m][:], WS, 1.0, ALU.mult, ALU.mult).then_inc(s["stage_up"], 1)
                        pool.wait_ge(s["stage_up"], now[m])
                        hi = (w1h, w2h)[m]
                        pool.tensor_tensor(lo[:, DS(i * F, F)], stage[m][:], hi[:, DS(i * F, F)],
                                           ALU.subtract).then_inc(s["stage_lo"], 1)
                    for b in range(2):
                        wait_att(s["att_ps"])
                        pool.tensor_copy(kt[b][:, 0:P], kt[b][:, P:2 * P])
                        pool.tensor_copy(vprev[b][:], val[b][:, 0:LD]).then_inc(s["prev_kept"], 1)

            @block.scalar
            def _(act):
                with act.Fori(0, NW) as i:
                    now, before = counts(act, i)
                    for b in range(2):
                        act.wait_ge(s["xnt"], now[b])
                        act.wait_ge(s["tok1"], before[b])
                        act.activation(xth[b][:], bA[b][:, 0:D], ACT.Copy, scale=XS).then_inc(s["xth_in"], 1)
                    for m, (hi, _lo) in enumerate(((w1h, w1l), (w2h, w2l))):
                        act.wait_ge(w_loaded[m], 16 * i + 16)
                        act.activation(hi[:, DS(i * F, F)], stage[m][:], ACT.Copy, scale=WS).then_inc(s["stage_hi"], 1)
                    for b in range(2):
                        act.wait_ge(s["tok1"], now[b])
                        act.wait_ge(s["prev_kept"], before[b])
                        act.activation(qt[b][:], bC[b][:, D:D + P], ACT.Copy,
                                       scale=-UN_XW * DH ** -0.5).then_inc(s["qt_in"], 1)
                        act.activation(kt[b][:, P:2 * P], bC[b][:, D + P:D + 2 * P], ACT.Copy,
                                       scale=UN_XW).then_inc(s["kt_in"], 1)
                        act.activation(val[b][:, 0:LD + GA], bC[b][:, 0:LD + GA], ACT.Copy, scale=UN_XW)
                        act.activation(val[b][:, LD + GA + 1:VC - 1], bC[b][:, LD + GA:D], ACT.Copy,
                                       scale=UN_XW).then_inc(s["v_in"], 1)
                    for b in range(2):
                        act.wait_ge(s["qsub_in"], now[b])
                        act.activation(qs[b][:, 0:GD], qs[b][:, 0:GD], ACT.Exp, scale=UN_XW).then_inc(s["qexp_in"], 1)
                        act.activation(ke[b][:, 0:GD], bB[b][:, CK:CK + GD], ACT.Exp, scale=UN_XW)
                        act.wait_ge(s["ke_in"], before[b])
                        act.activation(krelu[b][:], bB[b][:, CK:CK + GD], ACT.Relu, scale=UN_XW)
                        act.activation(scores[:, DS(b * NW + i, 1), :], bB[b][:, CR:CR + E], ACT.Copy,
                                       scale=UN_XW).then_inc(s["tok0_read"], 1)
                    for b in range(2):
                        act.wait_ge(s["negmax_in"], now[b])
                        for h in range(LH):
                            ins = act.activation(ss[b][:, h, :], ss[b][:, h, :], ACT.Exp, scale=-1.0,
                                                 bias=negmax[b][:, h:h + 1], accum_out=rsum[b][:, h:h + 1])
                        ins.then_inc(s["prob"], 1)
                    for b in range(2):
                        act.wait_ge(s["pt_ps"], now[b])
                        act.activation(pt[b][:, 2:4, :, :], bB[b][:].rearrange("p (h c n) -> p h c n", h=2, c=2),
                                       ACT.Copy).then_inc(s["ptb_in"], 1)
                    for b in range(2):
                        act.wait_ge(s["at_ps"], now[b])
                        act.activation(ath[b][:], bD[b][:, 0:D], ACT.Copy, scale=AS).then_inc(s["ath_in"], 1)

            @block.tensor
            def _(pe):
                with pe.Fori(0, NW) as i:
                    now, before = counts(pe, i)
                    for b in range(2):
                        pe.wait_ge(s["xn_in"], now[b])
                        pe.wait_ge(s["res_in"], before[b])
                        for k in range(KC):
                            ins = pe.transpose(bA[b][:, k * P:(k + 1) * P], xn[b][:, k * P:(k + 1) * P], ident[:])
                        ins.then_inc(s["xnt"], 1)
                    for b in range(2):
                        pe.wait_ge(s["xtl_in"], now[b])
                        pe.wait_ge(s["ptb_in"], before[b])
                        xt = (xth[b], xtl[b])
                        lhs = lambda a, k: xt[a][:, k * P:(k + 1) * P]
                        three(pe, bB[b][:, 0:CV], lhs, lambda c, k: wtok[c][:, k, 0:CV],
                              range(KC)).then_inc(s["tok0"], 1)
                        pe.wait_ge(s["attn_in"], before[b])
                        three(pe, bC[b][:, 0:D], lhs, lambda c, k: wtok[c][:, k, CV:NTOKC], range(KC))
                        for m in range(2):
                            ins = three(pe, bC[b][:, D + m * P:D + (m + 1) * P],
                                        lambda a, k: wqk[a][:, k, m, :, :].rearrange("p h e -> p (h e)"),
                                        lambda c, k: xt[c][:, k * P:(k + 1) * P], range(KC))
                        ins.then_inc(s["tok1"], 1)
                    for b in range(2):
                        pe.wait_ge(s["qt_in"], now[b])
                        pe.wait_ge(s["kt_in"], now[b])
                        pe.wait_ge(s["tok0_read"], now[b])
                        for h in (0, 2, 1, 3):
                            dst = (bA, bB)[h // 2][b]
                            c0 = (h % 2) * 2 * P
                            if h % 2:
                                pe.wait_ge(s[("head0", "head2")[h // 2]], now[b])
                            ins = pe.matmul(dst[:, c0:c0 + 2 * P], qt[b][32 * h:32 * h + DH, :],
                                            kt[b][32 * h:32 * h + DH, :], start=True, stop=True)
                            if h % 2 == 0:
                                ins.then_inc(s[("head0", "head2")[h // 2]], 1)
                        ins.then_inc(s["s_ps"], 1)
                    for b in range(2):
                        pe.wait_ge(s["qn_in"], now[b])
                        pe.wait_ge(s["atl_in"], before[b])
                        for g in range(2):
                            ins = pe.transpose(bD[b][:, g * P:(g + 1) * P], qs[b][:, g * P:(g + 1) * P], ident[:])
                        ins.then_inc(s["qgt_ps"], 1)
                        pe.wait_ge(s["ke_in"], now[b])
                        pe.wait_ge(s["v_in"], now[b])
                        for u, dst in ((0, bD[b][:, D:D + CTX]), (1, bC[b][:, 0:CTX])):
                            r = slice(64 * u, 64 * u + 64)
                            pe.matmul(dst[:, 0:GA + 1], ke[b][r, 0:GA], val[b][r, LD:LD + GA + 1],
                                      start=True, stop=True)
                            ins = pe.matmul(dst[:, GA + 1:CTX], ke[b][r, GA:2 * GA], val[b][r, LD + GA + 1:VC],
                                            start=True, stop=True)
                        ins.then_inc(s["ctx_ps"], 1)
                    for b in range(2):
                        pe.wait_ge(s["prob"], now[b])
                        pe.wait_ge(s["negmax_in"], now[b])
                        for h in range(LH):
                            for c in range(2):
                                c0 = (h % 2) * 2 * P + c * P
                                ins = pe.transpose((bA, bB)[h // 2][b][:, c0:c0 + P],
                                                   ss[b][:, h, c * P:(c + 1) * P], ident[:])
                        ins.then_inc(s["pt_ps"], 1)
                    for b in range(2):
                        pe.wait_ge(s["new_in"], now[b])
                        pe.wait_ge(s["pta_in"], now[b])
                        pe.wait_ge(s["ptb_in"], now[b])
                        for h in range(LH):
                            c0 = h * DH
                            pe.matmul(bC[b][:, c0:c0 + DH], pt[b][:, h, 0, :], vprev[b][:, c0:c0 + DH],
                                      start=True, stop=False)
                            pe.matmul(bC[b][:, c0:c0 + DH], pt[b][:, h, 1, :], val[b][:, c0:c0 + DH],
                                      start=False, stop=True)
                        pe.wait_ge(s["qgt_in"], now[b])
                        for u, state in enumerate((cum[b], cum0[b])):
                            r = slice(64 * u, 64 * u + 64)
                            pe.matmul(bC[b][r, LD:LD + GA], qgt[b][:, 0, r], state[:, 0:GA], start=True, stop=True)
                            ins = pe.matmul(bC[b][r, LD + GA:D], qgt[b][:, 1, r], state[:, GA + 1:GA + 1 + GB],
                                            start=True, stop=True)
                        ins.then_inc(s["att_ps"], 1)
                    for b in range(2):
                        pe.wait_ge(s["attn_in"], now[b])
                        for k in range(KC):
                            ins = pe.transpose(bD[b][:, k * P:(k + 1) * P], attn[b][:, k * P:(k + 1) * P], ident[:])
                        ins.then_inc(s["at_ps"], 1)
                    for b in range(2):
                        pe.wait_ge(s["atl_in"], now[b])
                        pe.wait_ge(s["pta_in"], now[b])
                        at = (ath[b], atl[b])
                        three(pe, bA[b][:, 0:D], lambda a, k: at[a][:, k * P:(k + 1) * P],
                              lambda c, k: wout[c][:, k, :], range(KC)).then_inc(s["pr_ps"], 1)

            @block.vector
            def _(dve):
                def spread(ap, n):
                    return ap.unsqueeze(len(ap.shape)).to_broadcast([*ap.shape, n])

                def heads(ap):
                    return ap.rearrange("p (h e) -> p h e", e=DH)

                wait_stats, wait_scores = stepper(dve, "stats_value", 3), stepper(dve, "scores_value", 3)
                with dve.Fori(0, NW) as i:
                    now, before = counts(dve, i)
                    for b in range(2):
                        dve.wait_ge(x_loaded[b], 16 * i + 16)
                        dve.bn_stats(stats[b][:], xin[b][:]).then_inc(s["stats_in"], 1)
                    for b in range(2):
                        wait_stats(s["stats_in"])
                        dve.bn_aggr(mv[b][:], stats[b][:]).then_inc(s["aggregated"], 1)
                    for b in range(2):
                        dve.wait_ge(s["aggregated"], now[b])
                        dve.tensor_scalar(veps[b][:], mv[b][:, 1:2], 1e-5, None, ALU.add).then_inc(s["veps_in"], 1)
                    for b in range(2):
                        dve.wait_ge(s["rstd_in"], now[b])
                        dve.wait_ge(s["xnt"], before[b])
                        dve.wait_ge(xn_stored[b], 16 * i + 16)
                        dve.tensor_scalar(xn[b][:], xin[b][:], mv[b][:, 0:1], rstd[b][:], ALU.subtract,
                                          ALU.mult).then_inc(s["xn_in"], 1)
                    for b in range(2):
                        dve.wait_ge(s["xth_in"], now[b])
                        dve.scalar_tensor_tensor(out=xtl[b][:], in0=bA[b][:, 0:D], scalar=XS, in1=xth[b][:],
                                                 op0=ALU.mult, op1=ALU.subtract).then_inc(s["xtl_in"], 1)
                    for b in range(2):
                        dve.wait_ge(s["tok0"], now[b])
                        dve.tensor_reduce(qmax[b][:], heads(bB[b][:, CQ:CQ + GD]), AX, ALU.max).then_inc(s["qmax_in"], 1)
                    for b in range(2):
                        dve.wait_ge(s["qmax_in"], now[b])
                        dve.wait_ge(s["qgt_ps"], before[b])
                        dve.tensor_tensor(heads(qs[b][:, 0:GD]), heads(bB[b][:, CQ:CQ + GD]), spread(qmax[b][:], DH),
                                          ALU.subtract).then_inc(s["qsub_in"], 1)
                    for b in range(2):
                        dve.wait_ge(s["qexp_in"], now[b])
                        dve.tensor_reduce(qsum[b][:], heads(qs[b][:, 0:GD]), AX, ALU.add).then_inc(s["qsum_in"], 1)
                    for b in range(2):
                        dve.wait_ge(s["tok0_read"], now[b])
                        dve.tensor_scalar(ke[b][:, 0:GD], ke[b][:, 0:GD], 1.0, None, ALU.min).then_inc(s["kexp_in"], 1)
                    for b in range(2):
                        dve.wait_ge(s["qsum_in"], now[b])
                        dve.reciprocal(qrec[b][:], qsum[b][:]).then_inc(s["qrec_in"], 1)
                    for b in range(2):
                        dve.wait_ge(s["qrec_in"], now[b])
                        dve.tensor_tensor(heads(qs[b][:, 0:GD]), heads(qs[b][:, 0:GD]), spread(qrec[b][:], DH),
                                          ALU.mult).then_inc(s["qn_in"], 1)
                    for b in range(2):
                        dve.wait_ge(s["mask_open"], before[1])
                        wait_scores(s["s_ps"])
                        for h in range(LH):
                            c0 = (h % 2) * 2 * P
                            ins = dve.tensor_tensor_reduce(ss[b][:, h, :], (bA, bB)[h // 2][b][:, c0:c0 + 2 * P],
                                                           causal[:], 1.0, BIG, ALU.add, ALU.min,
                                                           negmax[b][:, h:h + 1])
                        ins.then_inc(s["negmax_in"], 1)
                    for b in range(2):
                        dve.wait_ge(s["ctx_ps"], now[b])
                        dve.tensor_tensor(new0[b][:], bD[b][:, D:D + CTX], ctx_mask[:], ALU.mult)
                        dve.tensor_tensor(new1[b][:], bC[b][:, 0:CTX], ctx_mask[:], ALU.mult).then_inc(s["new_in"], 1)
                    dve.wait_ge(s["negmax_in"], now[1])
                    dve.memset(causal[:, 0:P], 0.0).then_inc(s["mask_open"], 2)
                    for b in range(2):
                        dve.wait_ge(s["new_in"], now[b])
                        dve.wait_ge(s["cum_in"], before[b])
                        dve.tensor_scalar(den[b][:, :, 0], cum[b][:, GA:CTX:GB + 1], 1e-6, None, ALU.add)
                        dve.tensor_tensor(cum0[b][:], cum[b][:], new0[b][:], ALU.add).then_inc(s["cum0_in"], 1)
                    for b in range(2):
                        dve.wait_ge(s["cum0_in"], now[b])
                        dve.tensor_scalar(den[b][:, :, 1], cum0[b][:, GA:CTX:GB + 1], 1e-6, None,
                                          ALU.add).then_inc(s["den_in"], 1)
                    for b in range(2):
                        dve.wait_ge(s["den_in"], now[b])
                        dve.reciprocal(rden[b][:], den[b][:]).then_inc(s["rden_in"], 1)
                    for b in range(2):
                        dve.wait_ge(s["rden_in"], now[b])
                        dve.tensor_tensor(qgt[b][:].rearrange("p g (u n) -> p g u n", u=2),
                                          bD[b][:, 0:D].rearrange("p (g u n) -> p g u n", g=2, u=2),
                                          spread(rden[b][:], P // 2), ALU.mult).then_inc(s["qgt_in"], 1)
                    for b in range(2):
                        dve.wait_ge(s["pt_ps"], now[b])
                        dve.tensor_copy(pt[b][:, 0:2, :, :], bA[b][:].rearrange("p (h c n) -> p h c n", h=2, c=2))\
                           .then_inc(s["pta_in"], 1)
                    for b in range(2):
                        dve.wait_ge(s["prob"], now[b])
                        dve.reciprocal(rrec[b][:], rsum[b][:]).then_inc(s["rrec_in"], 1)
                    for b in range(2):
                        dve.wait_ge(s["att_ps"], now[b])
                        dve.wait_ge(s["rrec_in"], now[b])
                        dve.tensor_tensor(heads(attn[b][:, 0:LD]), heads(bC[b][:, 0:LD]), spread(rrec[b][:], DH),
                                          ALU.mult)
                        dve.tensor_copy(attn[b][:, LD:D], bC[b][:, LD:D]).then_inc(s["attn_in"], 1)
                        dve.tensor_tensor(cum[b][:], cum0[b][:], new1[b][:], ALU.add).then_inc(s["cum_in"], 1)
                    for b in range(2):
                        dve.wait_ge(s["ath_in"], now[b])
                        dve.scalar_tensor_tensor(out=atl[b][:], in0=bD[b][:, 0:D], scalar=AS, in1=ath[b][:],
                                                 op0=ALU.mult, op1=ALU.subtract).then_inc(s["atl_in"], 1)
                    for b in range(2):
                        dve.wait_ge(s["pr_ps"], now[b])
                        dve.wait_ge(s["xb_in"], now[b])
                        dve.wait_ge(res_stored[b], 16 * i + 16)
                        dve.scalar_tensor_tensor(out=res[b][:], in0=bA[b][:, 0:D], scalar=UN_AW, in1=xb[b][:],
                                                 op0=ALU.mult, op1=ALU.add).then_inc(s["res_in"], 1)

        def view(t, off, *shape, dt=F32):
            n = 1
            for m in shape:
                n *= m
            flat = t[:].rearrange("p a b -> p (a b)") if len(t.shape) == 3 else (
                t[:].rearrange("p a b c -> p (a b c)") if len(t.shape) == 4 else t[:])
            if dt is F16:
                ap = flat[:, off:off + n // 2].bitcast(F16)
            else:
                ap = flat[:, off:off + n]
                if dt is not F32:
                    ap = ap.bitcast(dt)
            names = "abcd"[:len(shape)]
            if len(shape) == 1:
                return ap
            return ap.rearrange(f"p ({' '.join(names)}) -> p {' '.join(names)}",
                                **{c: m for c, m in zip(names[:-1], shape[:-1])})

        TE = NT * E
        eq, oh1, oh2, rest = (view(ss[0], c * TE, NT, E) for c in range(4))
        rank, prod, excl, tot = view(ss[1], 0, NT, E), view(ss[1], TE, NT, E), view(ss[1], 2 * TE, E, NT), view(ss[1], 3 * TE, E, NT)
        both = view(pt[0], 0, NT, E, dt=F16)
        incl = view(pt[0], TE, E, NT)
        tri, ones16 = view(pt[0], 2 * TE, P, dt=F16), view(pt[0], 2 * TE + P // 2, P, dt=F16)
        pos_iota, blk_iota = view(pt[0], 2 * TE + P, P, dt=F16), view(pt[0], 2 * TE + P + P // 2, NB, dt=F16)
        small = pt[1]
        c0 = 0
        sm = {}
        for name, shape, dt in (("m1", (NT,), F32), ("m2", (NT,), F32), ("pm", (NT,), F32), ("ed", (NT,), F32),
                                ("dn", (NT,), F32), ("gate", (NT, TOPK), F32), ("rk", (NT, TOPK), F32),
                                ("ri", (NT, TOPK), I32), ("rp", (NT, TOPK), I32), ("obk", (NT, TOPK), F32),
                                ("pos", (NT, TOPK), F32), ("blk", (NT, TOPK), F32), ("gh", (NT, TOPK), F16),
                                ("gh32", (NT, TOPK), F32), ("glo", (NT, TOPK), F32), ("order", (E,), F32), ("one", (NT,), F32),
                                ("pcol", (1,), F32), ("tcol", (NT,), F32)):
            n = 1
            for m in shape:
                n *= m
            sm[name] = view(small, c0, *shape, dt=dt)
            c0 += n if dt is not F16 else (n + 1) // 2
        nbk, nbi, incb, offb = view(xb[0], 0, E), view(xb[0], E, E, dt=I32), view(xb[0], 2 * E, E), view(xb[0], 3 * E, E)
        jiota = view(xb[0], 4 * E, NB)
        cmp = view(stage[0], 0, NB, E)
        onehot_pos = [view(xin[m], 0, TOPK, P, dt=F16) for m in range(2)]
        onehot_blk = [view(stage[1], m * 320, TOPK, 4, NB, dt=F16) for m in range(2)]
        slot_row = view(xn[0], 0, NB, dt=I32)
        slot_gate = view(xn[0], NB, NB)
        expert_of = view(xn[1], 0, NB, dt=I32)
        ta, tb = view(xn[1], NB, NB), view(xn[1], 2 * NB, NB)
        zeros = view(qgt[0], 0, 4 * NB, dt=F16)
        scr = scores[:]

        routed, rconst = sem("routed"), sem("rconst")
        gate_exp, counted, mapped = sem("gate_exp"), sem("counted"), sem("mapped")
        both_in, hot_in, hot_used = sem("both_in"), sem("hot_in"), sem("hot_used")
        zeros_in = sem("zeros_in")

        with nc.Block() as block:
            @block.gpsimd
            def _(pool):
                pool.memset(tri, 1.0).then_inc(rconst, 1)
                pool.memset(ones16, 1.0).then_inc(rconst, 1)
                pool.memset(sm["one"], 1.0).then_inc(rconst, 1)
                pool.iota(sm["order"], pattern=[[-1, E]], base=E, channel_multiplier=0,
                          allow_small_or_imprecise_dtypes=True).then_inc(rconst, 1)
                pool.iota(pos_iota, pattern=[[1, P]], base=0, channel_multiplier=0,
                          allow_small_or_imprecise_dtypes=True).then_inc(rconst, 1)
                pool.iota(blk_iota, pattern=[[1, NB]], base=0, channel_multiplier=0,
                          allow_small_or_imprecise_dtypes=True).then_inc(rconst, 1)
                pool.iota(jiota, pattern=[[1, NB]], base=0, channel_multiplier=0,
                          allow_small_or_imprecise_dtypes=True).then_inc(rconst, 1)
                pool.iota(sm["pcol"], pattern=[[0, 1]], base=0, channel_multiplier=1,
                          allow_small_or_imprecise_dtypes=True).then_inc(rconst, 1)
                pool.iota(sm["tcol"], pattern=[[1, NT]], base=-NT, channel_multiplier=0,
                          allow_small_or_imprecise_dtypes=True).then_inc(rconst, 1)
                pool.wait_ge(rconst, 9)
                pool.affine_select(out=tri, in_=tri, compare_op=ALU.is_gt, fill=0.0, base=0,
                                   pattern=[[1, P]], channel_multiplier=-1).then_inc(rconst, 1)

            @block.scalar
            def _(act):
                act.wait_ge(gate_exp, 1)
                act.activation(sm["ed"], sm["dn"], ACT.Exp).then_inc(gate_exp, 1)

            @block.tensor
            def _(pe):
                pe.wait_ge(rconst, 10)
                pe.sem_inc(hot_used, 2)
                pe.wait_ge(both_in, 1)
                flat = both.rearrange("p t e -> p (t e)")
                pe.matmul(bank[0][:, 0:TE], tri, flat, start=True, stop=True)
                pe.matmul(bank[1][:, 0:TE], ones16, flat, start=True, stop=True).then_inc(counted, 1)
                pe.wait_ge(zeros_in, 1)
                pe.matmul(bank[2][:, 0:4 * NB], zeros[:, 0:P], zeros, start=True, stop=False, skip_group_check=True)
                with pe.Fori(0, NT // 2) as i:
                    for m in range(2):
                        pe.wait_ge(hot_in, 2 * i + m + 1)
                        for c in range(TOPK):
                            ins = pe.matmul(bank[2][:, 0:4 * NB], onehot_pos[m][:, c, :],
                                            onehot_blk[m][:, c, :, :].rearrange("p v n -> p (v n)"),
                                            start=False, stop=False, skip_group_check=True)
                        ins.then_inc(hot_used, 1)
                pe.matmul(bank[2][:, 0:4 * NB], zeros[:, 0:P], zeros, start=False, stop=True,
                          skip_group_check=True).then_inc(mapped, 1)

            @block.vector
            def _(dve):
                done = [0]

                def then(ins):
                    done[0] += 1
                    ins.then_inc(routed, 1)
                    dve.wait_ge(routed, done[0])

                def per_token(ap):
                    return ap.unsqueeze(2).to_broadcast([P, NT, E])

                def per_expert(ap):
                    return ap.unsqueeze(1).to_broadcast([P, NT, E])

                def pick(src, top, onehot):
                    then(dve.tensor_reduce(top, src, AX, ALU.max))
                    then(dve.tensor_tensor(eq, src, per_token(top), ALU.is_equal))
                    then(dve.tensor_tensor(eq, eq, per_expert(sm["order"]), ALU.mult))
                    then(dve.tensor_reduce(sm["pm"], eq, AX, ALU.max))
                    then(dve.tensor_tensor(onehot, eq, per_token(sm["pm"]), ALU.is_equal))

                dve.memset(zeros, 0.0).then_inc(zeros_in, 1)
                dve.wait_ge(rconst, 10)
                pick(scr, sm["m1"], oh1)
                then(dve.scalar_tensor_tensor(out=rest, in0=oh1, scalar=-BIG, in1=scr, op0=ALU.mult, op1=ALU.add))
                pick(rest, sm["m2"], oh2)
                dve.tensor_tensor(both, oh1, oh2, ALU.add).then_inc(both_in, 1)
                dve.tensor_tensor(sm["dn"], sm["m2"], sm["m1"], ALU.subtract).then_inc(gate_exp, 1)
                dve.wait_ge(gate_exp, 2)
                then(dve.tensor_scalar(sm["m1"], sm["ed"], 1.0, None, ALU.add))
                then(dve.reciprocal(sm["gate"][:, :, 0], sm["m1"]))
                then(dve.tensor_tensor(sm["gate"][:, :, 1], sm["ed"], sm["gate"][:, :, 0], ALU.mult))
                then(dve.tensor_copy(sm["gh"], sm["gate"]))
                then(dve.tensor_copy(sm["gh32"], sm["gh"]))
                then(dve.tensor_tensor(sm["glo"], sm["gate"], sm["gh32"], ALU.subtract))
                then(dve.tensor_scalar(sm["glo"], sm["glo"], 2048.0, None, ALU.mult))
                dve.wait_ge(counted, 1)
                then(dve.tensor_copy(tot, bank[1][:, 0:TE].rearrange("p (t e) -> p e t", e=E)))
                for e in range(E):
                    last = dve.tensor_tensor_scan(incl[:, e, :], sm["one"], tot[:, e, :], 0.0, ALU.mult, ALU.add)
                then(last)
                then(dve.tensor_tensor(excl, incl, tot, ALU.subtract))
                then(dve.tensor_tensor(rank, bank[0][:, 0:TE].rearrange("p (t e) -> p t e", e=E),
                                       excl.rearrange("p e t -> p t e"), ALU.add))
                then(dve.tensor_scalar(nbi, incl[:, :, NT - 1], float(P - 1), None, ALU.add))
                then(dve.tensor_scalar(nbi, nbi, 7, None, ALU.arith_shift_right))
                then(dve.tensor_copy(nbk, nbi))
                then(dve.tensor_tensor_scan(incb, sm["one"][:, 0:E], nbk, 0.0, ALU.mult, ALU.add))
                then(dve.tensor_tensor(offb, incb, nbk, ALU.subtract))
                for c, onehot in enumerate((oh1, oh2)):
                    then(dve.tensor_tensor(prod, onehot, rank, ALU.mult))
                    then(dve.tensor_reduce(sm["rk"][:, :, c], prod, AX, ALU.add))
                    then(dve.tensor_tensor(prod, onehot, per_expert(offb), ALU.mult))
                    then(dve.tensor_reduce(sm["obk"][:, :, c], prod, AX, ALU.add))
                then(dve.tensor_copy(sm["ri"], sm["rk"]))
                then(dve.tensor_scalar(sm["rp"], sm["ri"], P - 1, None, ALU.bitwise_and))
                then(dve.tensor_copy(sm["pos"], sm["rp"]))
                then(dve.tensor_scalar(sm["rp"], sm["ri"], 7, None, ALU.arith_shift_right))
                then(dve.tensor_copy(sm["blk"], sm["rp"]))
                then(dve.tensor_tensor(sm["blk"], sm["blk"], sm["obk"], ALU.add))
                then(dve.tensor_tensor(cmp, incb.unsqueeze(1).to_broadcast([P, NB, E]),
                                       jiota.unsqueeze(2).to_broadcast([P, NB, E]), ALU.is_le))
                then(dve.tensor_reduce(ta, cmp, AX, ALU.add))
                then(dve.tensor_scalar(expert_of, ta, float(E - 1), None, ALU.min))
                with dve.Fori(0, NT // 2) as i:
                    for m in range(2):
                        t = dve.snap(2 * i + m)
                        col = lambda ap: ap[:, DS(t, 1)]
                        dve.wait_ge(hot_used, 2 * i + m + 1)
                        for c in range(TOPK):
                            dve.tensor_scalar(onehot_pos[m][:, c, :], pos_iota, col(sm["pos"][:, :, c]), None, ALU.is_equal)
                            vals = (col(sm["tcol"]), sm["pcol"], col(sm["gh32"][:, :, c]), col(sm["glo"][:, :, c]))
                            for v, value in enumerate(vals):
                                ins = dve.tensor_scalar(onehot_blk[m][:, c, v, :], blk_iota, col(sm["blk"][:, :, c]),
                                                        value, ALU.is_equal, ALU.mult)
                        ins.then_inc(hot_in, 1)
                dve.wait_ge(mapped, 1)
                table = bank[2][:, 0:4 * NB].rearrange("p (v n) -> p v n", v=4)
                dve.tensor_copy(slot_gate, table[:, 2, :])
                dve.tensor_scalar(tb, table[:, 0, :], 0.0, sm["pcol"], ALU.is_equal, ALU.mult)
                then(dve.tensor_scalar(ta, table[:, 0, :], float(P), float(TOK), ALU.mult, ALU.add))
                then(dve.tensor_tensor(ta, table[:, 1, :], ta, ALU.add))
                then(dve.tensor_tensor(slot_row, ta, tb, ALU.add))
                then(dve.scalar_tensor_tensor(out=slot_gate, in0=table[:, 3, :], scalar=1 / 2048.0, in1=slot_gate,
                                              op0=ALU.mult, op1=ALU.add))


        bX, bH, bG, bY = bank[0], bank[1:3], bank[3:5], bank[5:7]
        xg = [xin[m][:] for m in range(2)]
        hid = ss[0][:].rearrange("p h n -> p (h n)")
        hth, htl = view(pt[0], 0, F, dt=F16), view(pt[0], F // 2, F, dt=F16)
        yg = [res[m][:] for m in range(2)]
        names = "xgt xgh_in xgl_in h0 h1 hid0 hid1 ht0 ht1 hh0 hh1 hl0 hl1 y_ps y_in from_in to_in".split()
        e = {n: sem("e_" + n) for n in names}
        gathered = [sem(f"gathered{m}") for m in range(2)]
        scattered = [sem(f"scattered{m}") for m in range(2)]

        def blocks(run, emit, peeled, first=0):
            for j in range(first):
                emit(j // 2, j % 2)
            with run.Fori(first // 2, (NB - peeled) // 2) as i:
                for m in range(2):
                    emit(i, m)
            for j in range(NB - peeled, NB):
                emit(j // 2, j % 2)

        def upto(i, m, ahead=0):
            return 2 * i + (m + ahead + 3)

        def slot(i, m, ahead):
            return (m + ahead) % 2, i + (m + ahead) // 2

        def beyond(i, m, ahead):
            return isinstance(i, int) and 2 * i + m + ahead >= NB

        with nc.Block() as block:
            @block.gpsimd
            def _(pool):
                wait_rows, wait_y = stepper(pool, "rows_value", 1), stepper(pool, "y_value", 3)

                def gather(i, m, ahead):
                    if beyond(i, m, ahead):
                        return
                    n, _k = slot(i, m, ahead)
                    pool.wait_ge(e["from_in"], upto(i, m, ahead))
                    wait_rows(e["xgt"])
                    pool.indirect_dma_start(out=xg[n], out_offset=None, in_=xn_rows,
                                            in_offset=bass.IndirectOffsetOnAxis(ap=rows_from[n][:, 0:1], axis=0))\
                        .then_inc(gathered[n], 16)

                def step(i, m):
                    gather(i, m, 3)
                    n, k = slot(i, m, -1)
                    pool.wait_ge(e["to_in"], upto(i, m))
                    if not (isinstance(k, int) and k < 0):
                        pool.wait_ge(scattered[n], 16 * k + 16)
                    wait_y(e["y_in"])
                    pool.indirect_dma_start(out=out, in_=yg[m], in_offset=None, compute_op=ALU.add,
                                            out_offset=bass.IndirectOffsetOnAxis(ap=rows_to[m][:, 0:1], axis=0))\
                        .then_inc(scattered[m], 16)

                for n in range(3):
                    gather(0, n, 0)
                blocks(pool, step, 4, first=2)
                for m in range(2):
                    pool.wait_ge(scattered[m], 16 * (NB // 2))

            @block.tensor
            def _(pe):
                for n in ("xgt", "h0", "h1", "ht0", "ht1", "y_ps"):
                    pe.sem_inc(e[n], 2)

                def turn_rows(i, m, ahead):
                    if beyond(i, m, ahead):
                        return
                    n, k = slot(i, m, ahead)
                    pe.wait_ge(gathered[n], 16 * k + 16)
                    pe.wait_ge(e["xgl_in"], upto(i, m, ahead - 1))
                    for c in range(KC):
                        ins = pe.transpose(bX[:, c * P:(c + 1) * P], xg[n][:, c * P:(c + 1) * P], ident[:])
                    ins.then_inc(e["xgt"], 1)

                def first(i, m, ahead):
                    if beyond(i, m, ahead):
                        return
                    n, k = slot(i, m, ahead)
                    which = pe.value_load(expert_of[0:1, DS(2 * i + m + ahead, 1)], min_val=0, max_val=E - 1)
                    pe.wait_ge(e["xgl_in"], upto(i, m, ahead))
                    xt = (xth[n], xtl[n])
                    for half in range(2):
                        pe.wait_ge(e[f"hid{half}"], upto(i, m, ahead - 1))
                        three(pe, bH[half][:], lambda a, c: xt[a][:, c * P:(c + 1) * P],
                              lambda a, c: (w1h, w1l)[a][:, DS(which * (KC * F) + (c * F + half * 512), 512)],
                              range(KC)).then_inc(e[f"h{half}"], 1)

                def step(i, m):
                    for half in range(2):
                        pe.wait_ge(e[f"hid{half}"], upto(i, m))
                        pe.wait_ge(e[f"hl{half}"], upto(i, m, -1))
                        for c in range(4):
                            f0 = (4 * half + c) * P
                            ins = pe.transpose(bG[half][:, c * P:(c + 1) * P], hid[:, f0:f0 + P], ident[:])
                        ins.then_inc(e[f"ht{half}"], 1)
                    first(i, m, 1)
                    turn_rows(i, m, 2)
                    which = pe.value_load(expert_of[0:1, DS(2 * i + m, 1)], min_val=0, max_val=E - 1)
                    pe.wait_ge(e["y_in"], upto(i, m, -2))
                    terms = [(f, a, c) for f in range(FC) for a, c in ((0, 0), (0, 1), (1, 0))]
                    for k, (f, a, c) in enumerate(terms):
                        if k % (3 * FC // 2) == 0:
                            pe.wait_ge(e[f"hl{f // 4}"], upto(i, m))
                        ins = pe.matmul(bY[m][:, 0:D], (hth, htl)[a][:, f * P:(f + 1) * P],
                                        (w2h, w2l)[c][:, DS(which * (FC * D) + f * D, D)],
                                        start=(k == 0), stop=(k == len(terms) - 1))
                    ins.then_inc(e["y_ps"], 1)

                turn_rows(0, 0, 0)
                first(0, 0, 0)
                turn_rows(0, 1, 0)
                blocks(pe, step, 2)

            @block.scalar
            def _(act):
                for n in ("xgh_in", "hid0", "hid1", "hh0", "hh1"):
                    act.sem_inc(e[n], 2)

                def rows_hi(i, m, ahead):
                    if beyond(i, m, ahead):
                        return
                    n, _k = slot(i, m, ahead)
                    act.wait_ge(e["xgt"], upto(i, m, ahead))
                    act.wait_ge(e["h1"], upto(i, m, ahead - 2))
                    act.activation(xth[n][:], bX[:, 0:D], ACT.Copy, scale=XS).then_inc(e["xgh_in"], 1)

                def gelu(i, m, ahead):
                    if beyond(i, m, ahead):
                        return
                    for half in range(2):
                        act.wait_ge(e[f"h{half}"], upto(i, m, ahead))
                        act.wait_ge(e[f"ht{half}"], upto(i, m, ahead - 1))
                        act.activation(hid[:, half * 512:(half + 1) * 512], bH[half][:], ACT.Gelu,
                                       scale=UN_XW).then_inc(e[f"hid{half}"], 1)

                def step(i, m):
                    for half in range(2):
                        act.wait_ge(e[f"ht{half}"], upto(i, m))
                        act.wait_ge(e["y_ps"], upto(i, m, -1))
                        act.activation(hth[:, half * 512:(half + 1) * 512], bG[half][:], ACT.Copy,
                                       scale=HS).then_inc(e[f"hh{half}"], 1)
                    gelu(i, m, 1)
                    rows_hi(i, m, 2)

                rows_hi(0, 0, 0)
                gelu(0, 0, 0)
                rows_hi(0, 1, 0)
                blocks(act, step, 2)

            @block.vector
            def _(dve):
                for n in ("xgl_in", "hl0", "hl1", "y_in", "from_in", "to_in"):
                    dve.sem_inc(e[n], 2)

                def rows_of(i, m, ahead):
                    if beyond(i, m, ahead):
                        return
                    n, k = slot(i, m, ahead)
                    if not (isinstance(k, int) and k == 0):
                        dve.wait_ge(gathered[n], 16 * k)
                    dve.tensor_copy(rows_from[n][:], slot_row[:, DS(2 * i + m + ahead, 1)]).then_inc(e["from_in"], 1)

                def rows_lo(i, m, ahead):
                    if beyond(i, m, ahead):
                        return
                    n, _k = slot(i, m, ahead)
                    dve.wait_ge(e["xgh_in"], upto(i, m, ahead))
                    dve.scalar_tensor_tensor(out=xtl[n][:], in0=bX[:, 0:D], scalar=XS, in1=xth[n][:],
                                             op0=ALU.mult, op1=ALU.subtract).then_inc(e["xgl_in"], 1)

                def step(i, m):
                    rows_of(i, m, 3)
                    for half in range(2):
                        h = slice(half * 512, (half + 1) * 512)
                        dve.wait_ge(e[f"hh{half}"], upto(i, m))
                        dve.scalar_tensor_tensor(out=htl[:, h], in0=bG[half][:], scalar=HS, in1=hth[:, h],
                                                 op0=ALU.mult, op1=ALU.subtract).then_inc(e[f"hl{half}"], 1)
                    if not (isinstance(i, int) and i == 0):
                        dve.wait_ge(scattered[m], 16 * i)
                    dve.tensor_copy(rows_to[m][:], slot_row[:, DS(2 * i + m, 1)]).then_inc(e["to_in"], 1)
                    rows_lo(i, m, 2)
                    dve.wait_ge(e["y_ps"], upto(i, m))
                    dve.tensor_scalar(yg[m], bY[m][:, 0:D], slot_gate[:, DS(2 * i + m, 1)], UN_HW, ALU.mult,
                                      ALU.mult).then_inc(e["y_in"], 1)

                for n in range(3):
                    rows_of(0, n, 0)
                rows_lo(0, 0, 0)
                rows_lo(0, 1, 0)
                blocks(dve, step, 4, first=2)


def kernel(**inputs):
    import numpy as _np
    import concourse.bacc as _bacc
    from concourse import mybir as _mybir
    from concourse.bass_utils import run_bass_kernel_spmd as _run

    a = {n: _np.asarray(v) for n, v in inputs.items()}
    w1 = a["L0_ffn_expert_w1"].transpose(0, 2, 1)
    w2 = a["L0_ffn_expert_w2"].transpose(0, 2, 1)
    w2 = w2.reshape(E, 2, FC // 2, P, D).transpose(0, 1, 3, 2, 4)
    arrays = {
        "x": a["L0_attn_x"].reshape(TOK, D),
        "wq": a["L0_attn_Wq"], "wk": a["L0_attn_Wk"], "wv": a["L0_attn_Wv"], "wo": a["L0_attn_Wo"],
        "bo": a["L0_attn_bo"],
        "rwt": a["L0_ffn_router_w"].T,
        "w1c": w1.reshape(E * KC * P, F),
        "w2c": w2.reshape(E * 2 * P, FC // 2 * D),
    }
    arrays = {n: _np.ascontiguousarray(v) for n, v in arrays.items()}
    nc = _bacc.Bacc("TRN2", target_bir_lowering=False, num_devices=1)
    args = [nc.dram_tensor(n, v.shape, _mybir.dt.from_np(v.dtype), kind="ExternalInput").ap()
            for n, v in arrays.items()]
    out = nc.dram_tensor("out", (TOK + PAD, D), F32, kind="ExternalOutput").ap()
    block_kernel(nc, *args, out)
    got = _run(nc, [arrays], core_ids=[0]).results[0]["out"]
    return got[:TOK].reshape(B, SEQ, D)
```

```python
from contextlib import ExitStack

import concourse.bass as bass
from concourse import mybir

ALU = mybir.AluOpType
ACT = mybir.ActivationFunctionType
F32 = mybir.dt.float32
F16 = mybir.dt.float16
I32 = mybir.dt.int32
AX = mybir.AxisListType.X

P = 128
B, SEQ, D = 2, 2048, 256
TOK = B * SEQ
NT = TOK // P
NW = SEQ // P
HEADS, LH, DH = 16, 4, 16
GD = (HEADS - LH) * DH
LD = LH * DH
KC = D // P
E, F, TOPK = 8, 1024, 2
FC = F // P
G = 2 * P
NG = (TOK * TOPK + E * (G - 1)) // G
NB = G // P * NG
PAD = P
BIG = 3.0e38
XS, WS, HS, AS = 256.0, 64.0, 16.0, 64.0
QS = 16.0
UN_XW, UN_AW, UN_HW = 1 / (XS * WS), 1 / (AS * WS), 1 / (HS * WS)
CQ, CK, CR, CV = 0, GD, 2 * GD, 2 * GD + E
NTOKC = CV + D
GA, GB = 128, 64
CTX = GA + 1 + GB + 1
VC = LD + CTX
DS = bass.ds


def block_kernel(nc, x, wq, wk, wv, wo, bo, rwt, w1c, w2c, out):
    with ExitStack() as ctx:
        def sb(name, shape, dt=F32):
            return ctx.enter_context(nc.sbuf_tensor(name, shape, dt))

        def sem(name):
            return ctx.enter_context(nc.semaphore(name))

        def pair(name, shape, dt=F32):
            return [sb(f"{name}{b}", shape, dt) for b in range(2)]

        xn_rows = nc.dram_tensor("xn_rows", (TOK + PAD, D), F32).ap()

        w1h, w1l = sb("w1h", [P, E * KC * F], F16), sb("w1l", [P, E * KC * F], F16)
        w2h, w2l = sb("w2h", [P, E * FC * D], F16), sb("w2l", [P, E * FC * D], F16)
        stage = pair("stage", [P, F])
        wtok = [sb(f"wtok{n}", [P, KC, NTOKC], F16) for n in "hl"]
        wqk = [sb(f"wqk{n}", [P, KC, 2, LH, 2, DH], F16) for n in "hl"]
        wout = [sb(f"wout{n}", [P, KC, D], F16) for n in "hl"]
        ident = sb("ident", [P, P])
        causal = sb("causal", [P, 3 * P])
        ctx_mask = sb("ctx_mask", [P, CTX])
        bias = sb("bias", [P, D])
        minus_half = sb("minus_half", [P, 1])
        scores = sb("scores", [P, NT, E])

        xin, xn, xb = pair("xin", [P, D]), pair("xn", [P, D]), pair("xb", [P, D])
        stats, mv = pair("stats", [P, 6]), pair("mv", [P, 2])
        veps, rstd = pair("veps", [P, 1]), pair("rstd", [P, 1])
        xth, xtl = pair("xth", [P, D], F16), pair("xtl", [P, D], F16)
        low_row = sb("low_row", [P, LH + 1])
        qm, qt, kt = pair("qm", [P, P], F16), pair("qt", [P, P], F16), pair("kt", [P, 2, 2 * P], F16)
        val = [pair(f"val{b}_", [P, VC]) for b in range(2)]
        qmax, qsum, qrec = pair("qmax", [P, 12]), pair("qsum", [P, 12]), pair("qrec", [P, 12])
        qs, krelu, ke = pair("qs", [P, D]), pair("krelu", [P, GD]), pair("ke", [P, D])
        ss, pt = sb("ss", [P, LH, 2 * P]), sb("pt", [P, LH, 2, P])
        spare = pair("spare", [P, LH, 2 * P])
        negmax, rsum, rrec = pair("negmax", [P, LH]), pair("rsum", [P, LH]), pair("rrec", [P, LH])
        cum, cum0 = pair("cum", [P, CTX]), pair("cum0", [P, CTX])
        new0, new1 = pair("new0", [P, CTX]), pair("new1", [P, CTX])
        den, rden = pair("den", [P, 2, 2]), pair("rden", [P, 2, 2])
        qgt = pair("qgt", [P, 2, P])
        attn, res = pair("attn", [P, D]), pair("res", [P, D])
        rows_from, rows_to = pair("rows_from", [P, 2], I32), pair("rows_to", [P, 2], I32)
        ath, atl = pair("ath", [P, D], F16), pair("atl", [P, D], F16)

        bank = [ctx.enter_context(nc.psum_tensor(f"bank{n}", [P, 512], F32)) for n in range(8)]

        got_w, got_c = sem("got_w"), sem("got_c")
        pool_const, zeroed, padded = sem("pool_const"), sem("zeroed"), sem("padded")
        w_hi, w_lo = sem("w_hi"), sem("w_lo")

        names = ("stats_in aggregated veps_in rstd_in xn_in xb_in xnt xth_in xtl_in tok0 qk tok1 qm_in kh_in qt_in kt_in "
                 "v_in kneg_in kexp_in qmax_in qsub_in qexp_in tok0_read qsum_in qrec_in qn_in ke_in qgt_ps "
                 "head0 head1 head2 head3 negmax0 negmax1 prob0 prob1 pt_ps pta_in ptb_in ctx_ps new0_in new_in "
                 "cum0_in den_in rden_in qgt_in att_ps rrec_in lin_in attn_in cum_in at_ps ath_in atl_in pr_ps res_in "
                 "stage_up stage_hi stage_lo").split()
        opened = sem("opened")
        s = {n: sem(n) for n in names}
        x_loaded = [sem(f"x_loaded{b}") for b in range(2)]
        xn_stored = [sem(f"xn_stored{b}") for b in range(2)]
        res_stored = [sem(f"res_stored{b}") for b in range(2)]
        xb_loaded = [sem(f"xb_loaded{b}") for b in range(2)]
        w_loaded = [sem(f"w_loaded{b}") for b in range(2)]

        wsrc = {"q": ss[:, 0:2, :], "k": ss[:, 2:4, :], "v": spare[0][:, 0:2, :], "o": spare[0][:, 2:4, :]}
        rsrc = qs[0][:, 0:KC * E].rearrange("p (k e) -> p k e", k=KC)

        jobs = [(lambda n: wtok[n][:, :, CQ:CQ + GD], wsrc["q"][:, :, LD:D]),
                (lambda n: wtok[n][:, :, CK:CK + GD], wsrc["k"][:, :, LD:D]),
                (lambda n: wtok[n][:, :, CR:CR + E], rsrc),
                (lambda n: wtok[n][:, :, CV:CV + D], wsrc["v"]),
                (lambda n: wout[n][:], wsrc["o"])]
        for k in range(KC):
            for m, name in enumerate("qk"):
                for c in range(2):
                    jobs.append((lambda n, k=k, m=m, c=c: wqk[n][:, k, m, :, c, :],
                                 wsrc[name][:, k, 0:LD].rearrange("p (h e) -> p h e", e=DH)))

        with nc.Block() as block:
            @block.sync
            def _(sp):
                for b in range(2):
                    sp.dma_start(xin[b][:], x[b * SEQ:b * SEQ + P, :]).then_inc(x_loaded[b], 16)
                for name, w in (("q", wq), ("k", wk), ("v", wv), ("o", wo)):
                    sp.dma_start(wsrc[name], w.rearrange("(k p) n -> p k n", p=P)).then_inc(got_w, 16)
                sp.dma_start(rsrc, rwt.rearrange("(k p) n -> p k n", p=P)).then_inc(got_w, 16)
                sp.dma_start(bias[:], bo.partition_broadcast(P)).then_inc(got_c, 16)
                for m, w in enumerate((w1c, w2c)):
                    sp.dma_start(stage[m][:], w[0:P, :]).then_inc(w_loaded[m], 16)
                sp.wait_ge(zeroed, 1)
                sp.dma_start(xn_rows[TOK:TOK + PAD, :], xn[0][:]).then_inc(padded, 16)
                sp.dma_start(out[TOK:TOK + PAD, :], xn[0][:]).then_inc(padded, 16)
                sp.wait_ge(got_c, 16)
                sp.wait_ge(padded, 32)

            @block.gpsimd
            def _(pool):
                pool.memset(ident[:], 0.0).then_inc(pool_const, 1)
                pool.memset(causal[:, 0:2 * P], 0.0).then_inc(pool_const, 1)
                pool.memset(causal[:, 2 * P:3 * P], BIG).then_inc(pool_const, 1)
                pool.memset(ctx_mask[:], 1.0).then_inc(pool_const, 1)
                pool.memset(minus_half[:], -0.5).then_inc(pool_const, 1)
                pool.memset(low_row[:], -QS * UN_XW).then_inc(pool_const, 1)
                pool.wait_ge(pool_const, 6)
                pool.affine_select(out=ident[:], in_=ident[:], compare_op=ALU.not_equal, fill=1.0, base=0,
                                   pattern=[[-1, P]], channel_multiplier=1).then_inc(pool_const, 1)
                pool.affine_select(out=causal[:, P:2 * P], in_=causal[:, P:2 * P], compare_op=ALU.is_ge,
                                   fill=BIG, base=0, pattern=[[-1, P]], channel_multiplier=1).then_inc(pool_const, 1)
                step = 8
                for c0, width in ((0, GA), (GA + 1, GB)):
                    v = ctx_mask[:, c0:c0 + width].rearrange("p (h e) -> p h e", e=DH)
                    for base, mult, sign in ((0, 1, -DH), (DH - 1, -1, DH)):
                        pool.wait_ge(pool_const, step)
                        pool.affine_select(out=v, in_=v, compare_op=ALU.is_ge, fill=0.0, base=base,
                                           pattern=[[sign, width // DH], [0, DH]],
                                           channel_multiplier=mult).then_inc(pool_const, 1)
                        step += 1
                for base, mult, sign in ((-DH, 1, -32), (31, -1, 32)):
                    pool.wait_ge(pool_const, step)
                    pool.affine_select(out=low_row[:, 0:LH], in_=low_row[:, 0:LH], compare_op=ALU.is_ge, fill=0.0,
                                       base=base, pattern=[[sign, LH]], channel_multiplier=mult).then_inc(pool_const, 1)
                    step += 1

            @block.scalar
            def _(act):
                act.wait_ge(got_w, 80)
                for dst, src in jobs:
                    act.activation(dst(0), src, ACT.Copy, scale=WS).then_inc(w_hi, 1)

            @block.vector
            def _(dve):
                dve.memset(xn[0][:], 0.0).then_inc(zeroed, 1)
                for b in range(2):
                    dve.memset(kt[b][:], 0.0)
                    dve.memset(val[b][1][:, 0:LD], 0.0)
                    dve.memset(cum[b][:], 0.0)
                    dve.memset(ke[b][:, GD:D], 0.0)
                    for odd in range(2):
                        dve.memset(val[b][odd][:, LD + GA:LD + GA + 1], 1.0)
                        dve.memset(val[b][odd][:, VC - 1:VC], 1.0)
                for c, (dst, src) in enumerate(jobs):
                    dve.wait_ge(w_hi, c + 1)
                    dve.scalar_tensor_tensor(out=dst(1), in0=src, scalar=WS, in1=dst(0),
                                             op0=ALU.mult, op1=ALU.subtract).then_inc(w_lo, 1)
                dve.wait_ge(pool_const, 14)
                dve.tensor_reduce(low_row[:, LH:LH + 1], low_row[:, 0:LH], AX, ALU.add)
                dve.wait_ge(w_lo, len(jobs))
                for b in range(2):
                    dve.memset(qs[b][:, GD:D], 0.0)

        def stepper(eng, name, first):
            value = eng.alloc_register(name)
            eng.reg_mov(value, first)

            def wait(semaphore, written_out=None):
                if written_out is not None:
                    eng.wait_ge(semaphore, written_out)
                else:
                    eng.wait_ge(semaphore, value)
                    eng.reg_add(value, value, 1)
            return wait

        class Step:

            def __init__(self, eng, i, b, u=None):
                self.eng, self.i, self.b, self.u = eng, i, b, i % 2 if u is None else u

            def has(self, off):
                return not isinstance(self.i, int) or 0 <= 2 * self.i + self.b + off < NT

            def row(self, off):
                return (self.b + off) % 2

            def window(self, off):
                return self.i + (self.b + off) // 2

            def odd(self, off):
                return (self.u + (self.b + off) // 2) % 2

            def own(self, off):
                return slice(self.odd(off) * P, (self.odd(off) + 1) * P)

            def first_row(self, off):
                return (self.row(off) * NW + self.window(off)) * P

            def wait(self, semaphore, off):
                c = self.b + off + 1
                if isinstance(self.i, int):
                    if 2 * self.i + c > 0:
                        self.eng.wait_ge(semaphore, 2 * self.i + c)
                else:
                    self.eng.wait_ge(semaphore, 2 * self.i + c)

            def wait_dma(self, semaphores, off):
                k = self.window(off) + 1
                if not isinstance(k, int) or k > 0:
                    self.eng.wait_ge(semaphores[self.row(off)], 16 * k)

        HEAD = 4

        def tile_stepper(eng, name, off):
            wait = stepper(eng, name, HEAD + off + 1)
            return lambda semaphore, t: wait(semaphore, 2 * t.i + t.b + off + 1 if isinstance(t.i, int) else None)

        def steps(eng, emit):
            for t in range(HEAD):
                emit(Step(eng, t // 2, t % 2))
            with eng.Fori(HEAD // 4, (NT - 4) // 4) as n:
                for t in range(4):
                    emit(Step(eng, 2 * n + t // 2, t % 2, t // 2))
            for t in range(NT - 4, NT + 3):
                emit(Step(eng, t // 2, t % 2))

        def three(pe, dst, lhs, rhs, chunks):
            terms = [(k, a, c) for k in chunks for a, c in ((0, 0), (0, 1), (1, 0))]
            for n, (k, a, c) in enumerate(terms):
                ins = pe.matmul(dst, lhs(a, k), rhs(c, k), start=(n == 0), stop=(n == len(terms) - 1))
            return ins

        b_xnt, b_tok0, b_tok1, b_s, b_ctx, b_att, b_out = bank[0], bank[1], bank[2], bank[3:5], bank[5], bank[6], bank[7]

        with nc.Block() as block:
            @block.sync
            def _(sp):
                def load_x(t, off):
                    sp.dma_start(xin[t.row(off)][:], x[DS(t.first_row(off), P), :]).then_inc(x_loaded[t.row(off)], 16)

                def load_weights(t, off):
                    m, w = t.row(off), (w1c, w2c)[t.row(off)]
                    sp.dma_start(stage[m][:], w[DS(t.window(off) * P, P), :]).then_inc(w_loaded[m], 16)

                def store_xn(t, off):
                    b = t.row(off)
                    t.wait(s["xn_in"], off)
                    sp.dma_start(xn_rows[DS(t.first_row(off), P), :], xn[b][:]).then_inc(xn_stored[b], 16)

                def step(t):
                    if t.has(-3):
                        b = t.row(-3)
                        t.wait(s["res_in"], -3)
                        sp.dma_start(out[DS(t.first_row(-3), P), :], res[b][:]).then_inc(res_stored[b], 16)
                    if t.has(-2):
                        b = t.row(-2)
                        t.wait(s["res_in"], -4)
                        sp.dma_start(xb[b][:], x[DS(t.first_row(-2), P), :]).then_inc(xb_loaded[b], 16)
                    if t.has(1):
                        store_xn(t, 1)
                    if t.has(3):
                        load_x(t, 3)
                    if t.has(2):
                        t.wait(s["stage_lo"], 0)
                        load_weights(t, 2)

                first = Step(sp, 0, 0)
                store_xn(first, 0)
                load_x(first, 2)
                steps(sp, step)
                for b in range(2):
                    sp.wait_ge(xn_stored[b], 16 * NW)
                    sp.wait_ge(res_stored[b], 16 * NW)

            @block.gpsimd
            def _(pool):
                wait_hi = tile_stepper(pool, "hi_value", 0)

                def step(t):
                    if t.has(-1):
                        b = t.row(-1)
                        t.wait(s["kexp_in"], -1)
                        pool.tensor_tensor(ke[b][:, 0:GD], ke[b][:, 0:GD], krelu[b][:], ALU.add).then_inc(s["ke_in"], 1)
                    if t.has(1):
                        rstd_of(t, 1)
                    if t.has(-2):
                        b = t.row(-2)
                        t.wait(s["new_in"], -2)
                        t.wait(s["att_ps"], -2)
                        pool.tensor_tensor(cum[b][:], cum0[b][:], new1[b][:], ALU.add).then_inc(s["cum_in"], 1)
                        t.wait_dma(xb_loaded, -2)
                        pool.tensor_tensor(xb[b][:], xb[b][:], bias[:], ALU.add).then_inc(s["xb_in"], 1)
                    if t.has(0):
                        m = t.row(0)
                        hi, lo = ((w1h, w1l), (w2h, w2l))[m]
                        wait_hi(s["stage_hi"], t)
                        pool.tensor_scalar(stage[m][:], stage[m][:], WS, 1.0, ALU.mult, ALU.mult).then_inc(s["stage_up"], 1)
                        t.wait(s["stage_up"], 0)
                        pool.tensor_tensor(lo[:, DS(t.window(0) * F, F)], stage[m][:], hi[:, DS(t.window(0) * F, F)],
                                           ALU.subtract).then_inc(s["stage_lo"], 1)

                def rstd_of(t, off):
                    b = t.row(off)
                    t.wait(s["veps_in"], off)
                    pool.tensor_tensor(rstd[b][:], veps[b][:], minus_half[:], ALU.pow).then_inc(s["rstd_in"], 1)

                rstd_of(Step(pool, 0, 0), 0)
                steps(pool, step)

            @block.scalar
            def _(act):
                def step(t):
                    if t.has(0):
                        b = t.row(0)
                        t.wait(s["xnt"], 0)
                        t.wait(s["tok1"], -2)
                        act.activation(xth[b][:], b_xnt[:, 0:D], ACT.Copy, scale=XS).then_inc(s["xth_in"], 1)
                        hi = (w1h, w2h)[b]
                        t.wait_dma(w_loaded, 0)
                        act.activation(hi[:, DS(t.window(0) * F, F)], stage[b][:], ACT.Copy, scale=WS)\
                            .then_inc(s["stage_hi"], 1)
                    if t.has(-2):
                        b = t.row(-2)
                        t.wait(s["att_ps"], -2)
                        t.wait(s["at_ps"], -4)
                        act.activation(attn[b][:, LD:D], b_att[:, LD:D], ACT.Copy).then_inc(s["lin_in"], 1)
                    for half in range(2):
                        if t.has(-1):
                            b = t.row(-1)
                            t.wait(s[f"negmax{half}"], -1)
                            t.wait(s["rrec_in"], -3)
                            for h in range(2 * half, 2 * half + 2):
                                ins = act.activation(ss[:, h, :], ss[:, h, :], ACT.Exp, scale=-1.0,
                                                     bias=negmax[b][:, h:h + 1], accum_out=rsum[b][:, h:h + 1])
                            ins.then_inc(s[f"prob{half}"], 1)
                        if half == 0 and t.has(-2):
                            b = t.row(-2)
                            t.wait(s["at_ps"], -2)
                            t.wait(s["pr_ps"], -4)
                            act.activation(ath[b][:], b_out[:, 0:D], ACT.Copy, scale=AS).then_inc(s["ath_in"], 1)
                    if t.has(0):
                        b = t.row(0)
                        t.wait(s["qk"], 0)
                        t.wait(s["qt_in"], -2)
                        act.activation(qm[b][:], b_xnt[:, D:D + P], ACT.Copy,
                                       scale=low_row[:, LH:LH + 1]).then_inc(s["qm_in"], 1)
                        t.wait(s["head3"], -2)
                        act.activation(kt[b][:, 0, t.own(0)], b_xnt[:, D + P:D + 2 * P], ACT.Copy,
                                       scale=QS * UN_XW).then_inc(s["kh_in"], 1)
                        t.wait(s["qsub_in"], 0)
                        act.activation(qs[b][:, 0:GD], qs[b][:, 0:GD], ACT.Exp, scale=UN_XW).then_inc(s["qexp_in"], 1)
                    if t.has(-1):
                        t.wait(s["pt_ps"], -1)
                        t.wait(s["att_ps"], -2)
                        act.activation(pt[:, 2:4, :, :], b_s[1][:].rearrange("p (h c n) -> p h c n", h=2, c=2),
                                       ACT.Copy).then_inc(s["ptb_in"], 1)
                    if t.has(0):
                        b = t.row(0)
                        t.wait(s["ctx_ps"], -2)
                        act.activation(ke[b][:, 0:GD], b_tok0[:, CK:CK + GD], ACT.Relu, scale=-UN_XW)\
                            .then_inc(s["kneg_in"], 1)
                        t.wait(s["ke_in"], -2)
                        act.activation(krelu[b][:], b_tok0[:, CK:CK + GD], ACT.Relu, scale=UN_XW)
                        act.activation(scores[:, DS(b * NW + t.window(0), 1), :], b_tok0[:, CR:CR + E], ACT.Copy,
                                       scale=UN_XW).then_inc(s["tok0_read"], 1)
                        t.wait(s["kneg_in"], 0)
                        act.activation(ke[b][:, 0:GD], ke[b][:, 0:GD], ACT.Exp, scale=-1.0).then_inc(s["kexp_in"], 1)
                        t.wait(s["att_ps"], -2)
                        t.wait(s["tok1"], 0)
                        v = val[b][t.odd(0)]
                        act.activation(v[:, 0:LD + GA], b_tok1[:, 0:LD + GA], ACT.Copy, scale=UN_XW)
                        act.activation(v[:, LD + GA + 1:VC - 1], b_tok1[:, LD + GA:D], ACT.Copy,
                                       scale=UN_XW).then_inc(s["v_in"], 1)

                steps(act, step)

            @block.tensor
            def _(pe):
                def step(t):
                    if t.has(-3):
                        b = t.row(-3)
                        t.wait(s["atl_in"], -3)
                        at = (ath[b], atl[b])
                        three(pe, b_out[:, D:2 * D], lambda a, k: at[a][:, k * P:(k + 1) * P],
                              lambda c, k: wout[c][:, k, :], range(KC)).then_inc(s["pr_ps"], 1)
                    if t.has(0):
                        b = t.row(0)
                        t.wait(s["xn_in"], 0)
                        t.wait(s["kt_in"], -1)
                        for k in range(KC):
                            ins = pe.transpose(b_xnt[:, k * P:(k + 1) * P], xn[b][:, k * P:(k + 1) * P], ident[:])
                        ins.then_inc(s["xnt"], 1)
                    if t.has(-1):
                        t.wait(s["kt_in"], -1)
                    if t.has(-2):
                        t.wait(s["ptb_in"], -2)
                        t.wait(s["pta_in"], -2)
                    for h in range(LH):
                        if h % 2 and t.has(-1):
                            t.wait(s[f"head{h - 1}"], -1)
                        for a in range(2):
                            if t.has(-1):
                                b, c0, r = t.row(-1), (h % 2) * 2 * P, slice(32 * h, 32 * h + 32)
                                ins = pe.matmul(b_s[h // 2][:, c0:c0 + 2 * P], qt[b][r, :], kt[b][r, a, :],
                                                start=(a == 0), stop=(a == 1))
                                if a == 1:
                                    ins.then_inc(s[f"head{h}"], 1)
                            if t.has(-2):
                                b, c = t.row(-2), slice(h * DH, (h + 1) * DH)
                                pe.matmul(b_att[:, c], pt[:, h, a, :], val[b][a][:, c],
                                          start=(a == 0), stop=(a == 1))
                    if t.has(-2):
                        b = t.row(-2)
                        t.wait(s["qgt_in"], -2)
                        for u, state in enumerate((cum[b], cum0[b])):
                            r = slice(64 * u, 64 * u + 64)
                            pe.matmul(b_att[r, LD:LD + GA], qgt[b][:, 0, r], state[:, 0:GA], start=True, stop=True)
                            ins = pe.matmul(b_att[r, LD + GA:D], qgt[b][:, 1, r], state[:, GA + 1:GA + 1 + GB],
                                            start=True, stop=True)
                        ins.then_inc(s["att_ps"], 1)
                    if t.has(-1):
                        b = t.row(-1)
                        t.wait(s["qn_in"], -1)
                        t.wait(s["qgt_in"], -2)
                        for g in range(2):
                            ins = pe.transpose(b_ctx[:, g * P:(g + 1) * P], qs[b][:, g * P:(g + 1) * P], ident[:])
                        ins.then_inc(s["qgt_ps"], 1)
                        t.wait(s["ke_in"], -1)
                        t.wait(s["v_in"], -1)
                        v = val[b][t.odd(-1)]
                        for u, dst in ((0, b_ctx[:, D:D + CTX]), (1, b_tok1[:, D:D + CTX])):
                            r = slice(64 * u, 64 * u + 64)
                            pe.matmul(dst[:, 0:GA + 1], ke[b][r, 0:GA], v[r, LD:LD + GA + 1],
                                      start=True, stop=True)
                            ins = pe.matmul(dst[:, GA + 1:CTX], ke[b][r, GA:2 * GA], v[r, LD + GA + 1:VC],
                                            start=True, stop=True)
                        ins.then_inc(s["ctx_ps"], 1)
                    if t.has(-2):
                        b = t.row(-2)
                        t.wait(s["attn_in"], -2)
                        t.wait(s["res_in"], -3)
                        for k in range(KC):
                            ins = pe.transpose(b_out[:, k * P:(k + 1) * P], attn[b][:, k * P:(k + 1) * P], ident[:])
                        ins.then_inc(s["at_ps"], 1)
                    if t.has(0):
                        b = t.row(0)
                        t.wait(s["xtl_in"], 0)
                        t.wait(s["tok0_read"], -1)
                        xt = (xth[b], xtl[b])
                        lhs = lambda a, k: xt[a][:, k * P:(k + 1) * P]
                        three(pe, b_tok0[:, 0:CV], lhs, lambda c, k: wtok[c][:, k, 0:CV],
                              range(KC)).then_inc(s["tok0"], 1)
                        for m in range(2):
                            ins = three(pe, b_xnt[:, D + m * P:D + (m + 1) * P],
                                        lambda a, k: wqk[a][:, k, m, :, :, :].rearrange("p h c e -> p (h c e)"),
                                        lambda c, k: xt[c][:, k * P:(k + 1) * P], range(KC))
                        ins.then_inc(s["qk"], 1)
                    if t.has(-1):
                        for half in range(2):
                            t.wait(s[f"prob{half}"], -1)
                            for h in range(2 * half, 2 * half + 2):
                                for c in range(2):
                                    c0 = (h % 2) * 2 * P + c * P
                                    ins = pe.transpose(b_s[half][:, c0:c0 + P], ss[:, h, c * P:(c + 1) * P], ident[:])
                        ins.then_inc(s["pt_ps"], 1)
                    if t.has(0):
                        t.wait(s["v_in"], -1)
                        t.wait(s["new_in"], -1)
                        three(pe, b_tok1[:, 0:D], lhs, lambda c, k: wtok[c][:, k, CV:NTOKC],
                              range(KC)).then_inc(s["tok1"], 1)
                steps(pe, step)

            @block.vector
            def _(dve):
                def spread(ap, n):
                    return ap.unsqueeze(len(ap.shape)).to_broadcast([*ap.shape, n])

                def heads(ap):
                    return ap.rearrange("p (h e) -> p h e", e=DH)

                wait_stats = tile_stepper(dve, "stats_value", 1)
                wait_scores = [tile_stepper(dve, f"scores{half}_value", -1) for half in range(2)]

                def mean_of(t, off):
                    b = t.row(off)
                    t.wait_dma(x_loaded, off)
                    dve.bn_stats(stats[b][:], xin[b][:]).then_inc(s["stats_in"], 1)

                def variance_of(t, off):
                    b = t.row(off)
                    if off:
                        wait_stats(s["stats_in"], t)
                    dve.bn_aggr(mv[b][:], stats[b][:]).then_inc(s["aggregated"], 1)
                    t.wait(s["aggregated"], off)
                    dve.tensor_scalar(veps[b][:], mv[b][:, 1:2], 1e-5, None, ALU.add).then_inc(s["veps_in"], 1)

                def normed(t, off):
                    b = t.row(off)
                    t.wait(s["rstd_in"], off)
                    t.wait(s["xnt"], off - 2)
                    t.wait_dma(xn_stored, off - 2)
                    dve.tensor_scalar(xn[b][:], xin[b][:], mv[b][:, 0:1], rstd[b][:], ALU.subtract,
                                      ALU.mult).then_inc(s["xn_in"], 1)

                def masked(t, half):
                    wait_scores[half](s[f"head{2 * half + 1}"], t)
                    mask = causal[:, 0:2 * P] if t.odd(-1) else causal[:, P:3 * P]
                    for h in (2 * half, 2 * half + 1):
                        c0 = (h % 2) * 2 * P
                        ins = dve.tensor_tensor_reduce(ss[:, h, :], b_s[half][:, c0:c0 + 2 * P], mask,
                                                       DH ** -0.5 / QS ** 2, BIG, ALU.add, ALU.min,
                                                       negmax[t.row(-1)][:, h:h + 1])
                    ins.then_inc(s[f"negmax{half}"], 1)

                def step(t):
                    if t.has(-3):
                        b = t.row(-3)
                        t.wait(s["pr_ps"], -3)
                        t.wait(s["xb_in"], -3)
                        t.wait_dma(res_stored, -5)
                        dve.scalar_tensor_tensor(out=res[b][:], in0=b_out[:, D:2 * D], scalar=UN_AW, in1=xb[b][:],
                                                 op0=ALU.mult, op1=ALU.add).then_inc(s["res_in"], 1)
                    if t.has(0):
                        b = t.row(0)
                        t.wait(s["xth_in"], 0)
                        dve.scalar_tensor_tensor(out=xtl[b][:], in0=b_xnt[:, 0:D], scalar=XS, in1=xth[b][:],
                                                 op0=ALU.mult, op1=ALU.subtract).then_inc(s["xtl_in"], 1)
                    if t.has(1):
                        mean_of(t, 1)
                    if t.has(1):
                        variance_of(t, 1)
                    if t.has(-1):
                        t.wait(s["pt_ps"], -2)
                        masked(t, 0)
                    if t.has(-2):
                        b = t.row(-2)
                        t.wait(s["prob1"], -2)
                        dve.reciprocal(rrec[b][:], rsum[b][:]).then_inc(s["rrec_in"], 1)
                    if t.has(-2):
                        b = t.row(-2)
                        t.wait(s["rrec_in"], -2)
                        t.wait(s["lin_in"], -2)
                        dve.tensor_tensor(heads(attn[b][:, 0:LD]), heads(b_att[:, 0:LD]), spread(rrec[b][:], DH),
                                          ALU.mult).then_inc(s["attn_in"], 1)
                    if t.has(-1):
                        b = t.row(-1)
                        masked(t, 1)
                        t.wait(s["ctx_ps"], -1)
                        t.wait(s["cum_in"], -3)
                        dve.tensor_tensor(new0[b][:], b_ctx[:, D:D + CTX], ctx_mask[:], ALU.mult).then_inc(s["new0_in"], 1)
                        dve.tensor_tensor(new1[b][:], b_tok1[:, D:D + CTX], ctx_mask[:], ALU.mult).then_inc(s["new_in"], 1)
                        dve.tensor_scalar(den[b][:, :, 0], cum[b][:, GA:CTX:GB + 1], 1e-6, None, ALU.add)
                        t.wait(s["new0_in"], -1)
                        dve.tensor_tensor(cum0[b][:], cum[b][:], new0[b][:], ALU.add).then_inc(s["cum0_in"], 1)
                    if t.has(-2):
                        b = t.row(-2)
                        t.wait(s["ath_in"], -2)
                        dve.scalar_tensor_tensor(out=atl[b][:], in0=b_out[:, 0:D], scalar=AS, in1=ath[b][:],
                                                 op0=ALU.mult, op1=ALU.subtract).then_inc(s["atl_in"], 1)
                    if t.has(-1):
                        b = t.row(-1)
                        t.wait(s["cum0_in"], -1)
                        dve.tensor_scalar(den[b][:, :, 1], cum0[b][:, GA:CTX:GB + 1], 1e-6, None,
                                          ALU.add).then_inc(s["den_in"], 1)
                    if t.has(1):
                        normed(t, 1)
                    if t.has(-1):
                        b = t.row(-1)
                        t.wait(s["den_in"], -1)
                        dve.reciprocal(rden[b][:], den[b][:]).then_inc(s["rden_in"], 1)
                    if t.has(0):
                        b = t.row(0)
                        t.wait(s["tok0"], 0)
                        dve.tensor_reduce(qmax[b][:], heads(b_tok0[:, CQ:CQ + GD]), AX, ALU.max).then_inc(s["qmax_in"], 1)
                    if t.has(-1):
                        b = t.row(-1)
                        t.wait(s["rden_in"], -1)
                        dve.tensor_tensor(qgt[b][:].rearrange("p g (u n) -> p g u n", u=2),
                                          b_ctx[:, 0:D].rearrange("p (g u n) -> p g u n", g=2, u=2),
                                          spread(rden[b][:], P // 2), ALU.mult).then_inc(s["qgt_in"], 1)
                    if t.has(0):
                        b = t.row(0)
                        t.wait(s["qmax_in"], 0)
                        t.wait(s["qgt_ps"], -2)
                        dve.tensor_tensor(heads(qs[b][:, 0:GD]), heads(b_tok0[:, CQ:CQ + GD]), spread(qmax[b][:], DH),
                                          ALU.subtract).then_inc(s["qsub_in"], 1)
                    if isinstance(t.i, int) and 2 * t.i + t.b == 2:
                        t.wait(s["negmax1"], -1)
                        dve.memset(causal[:, 2 * P:3 * P], 0.0).then_inc(opened, 1)
                        dve.wait_ge(opened, 1)
                    if t.has(0):
                        b = t.row(0)
                        t.wait(s["kh_in"], 0)
                        t.wait(s["head3"], -2)
                        dve.scalar_tensor_tensor(out=qt[b][:], in0=b_xnt[:, D:D + P], scalar=-QS * UN_XW, in1=qm[b][:],
                                                 op0=ALU.mult, op1=ALU.subtract).then_inc(s["qt_in"], 1)
                        dve.scalar_tensor_tensor(out=kt[b][:, 1, t.own(0)], in0=b_xnt[:, D + P:D + 2 * P],
                                                 scalar=QS * UN_XW, in1=kt[b][:, 0, t.own(0)],
                                                 op0=ALU.mult, op1=ALU.subtract).then_inc(s["kt_in"], 1)
                    if t.has(-1):
                        t.wait(s["pt_ps"], -1)
                        t.wait(s["att_ps"], -2)
                        dve.tensor_copy(pt[:, 0:2, :, :], b_s[0][:].rearrange("p (h c n) -> p h c n", h=2, c=2))\
                           .then_inc(s["pta_in"], 1)
                    if t.has(0):
                        b = t.row(0)
                        t.wait(s["qexp_in"], 0)
                        dve.tensor_reduce(qsum[b][:], heads(qs[b][:, 0:GD]), AX, ALU.add).then_inc(s["qsum_in"], 1)
                        t.wait(s["qsum_in"], 0)
                        dve.reciprocal(qrec[b][:], qsum[b][:]).then_inc(s["qrec_in"], 1)
                        t.wait(s["qrec_in"], 0)
                        dve.tensor_tensor(heads(qs[b][:, 0:GD]), heads(qs[b][:, 0:GD]), spread(qrec[b][:], DH),
                                          ALU.mult).then_inc(s["qn_in"], 1)

                first = Step(dve, 0, 0)
                mean_of(first, 0)
                dve.wait_ge(s["stats_in"], 1)
                variance_of(first, 0)
                normed(first, 0)
                steps(dve, step)

        def view(t, off, *shape, dt=F32):
            n = 1
            for m in shape:
                n *= m
            flat = t[:].rearrange("p a b -> p (a b)") if len(t.shape) == 3 else (
                t[:].rearrange("p a b c -> p (a b c)") if len(t.shape) == 4 else t[:])
            if dt is F16:
                ap = flat[:, off:off + n // 2].bitcast(F16)
            else:
                ap = flat[:, off:off + n]
                if dt is not F32:
                    ap = ap.bitcast(dt)
            names = "abcd"[:len(shape)]
            if len(shape) == 1:
                return ap
            return ap.rearrange(f"p ({' '.join(names)}) -> p {' '.join(names)}",
                                **{c: m for c, m in zip(names[:-1], shape[:-1])})

        TE = NT * E
        eq, oh1, oh2, rest = (view(ss, c * TE, NT, E) for c in range(4))
        rank, prod, excl, tot = view(spare[0], 0, NT, E), view(spare[0], TE, NT, E), view(spare[0], 2 * TE, E, NT), view(spare[0], 3 * TE, E, NT)
        both = view(pt, 0, NT, E, dt=F16)
        incl = view(pt, TE, E, NT)
        tri, ones16 = view(pt, 2 * TE, P, dt=F16), view(pt, 2 * TE + P // 2, P, dt=F16)
        pos_iota, blk_iota = view(pt, 2 * TE + P, P), view(pt, 2 * TE + 2 * P, NB)
        small = spare[1]
        c0 = 0
        sm = {}
        for name, shape, dt in (("m1", (NT,), F32), ("m2", (NT,), F32), ("pm", (NT,), F32), ("ed", (NT,), F32),
                                ("dn", (NT,), F32), ("val", (NT, TOPK, 2), F32), ("rk", (NT, TOPK), F32),
                                ("ri", (NT, TOPK), I32), ("rp", (NT, TOPK), I32), ("obk", (NT, TOPK), F32),
                                ("pos", (NT * TOPK,), F32), ("blk", (NT * TOPK,), F32), ("order", (E,), F32),
                                ("one", (NT,), F32), ("pcol", (1,), F32), ("tok", (NT,), F32)):
            n = 1
            for m in shape:
                n *= m
            sm[name] = view(small, c0, *shape, dt=dt)
            c0 += n if dt is not F16 else (n + 1) // 2
        nbk, nbi, incb, offb = view(xb[0], 0, E), view(xb[0], E, E, dt=I32), view(xb[0], 2 * E, E), view(xb[0], 3 * E, E)
        jiota = view(xb[0], 4 * E, NG)
        cmp = view(stage[0], 0, NG, E)
        CH = 4
        onehot_pos = [view(spare[0], m * CH * P, CH, P) for m in range(2)]
        onehot_blk = [view(stage[m], 0, CH, NB) for m in range(2)]
        blk_vals = [view(stage[m], CH * NB, CH, 2, NB) for m in range(2)]
        slot_row = view(xn[0], 0, NB, dt=I32)
        slot_gate = view(xn[0], NB, NB)
        expert_of = view(xn[1], 0, NG, dt=I32)
        ta, tb = view(xn[1], NB, NB), view(xn[1], 2 * NB, NB)
        zeros = view(qgt[0], 0, 2 * NB, dt=F16)
        scr = scores[:]

        routed, rconst = sem("routed"), sem("rconst")
        gate_exp, counted, mapped = sem("gate_exp"), sem("counted"), sem("mapped")
        both_in, val_in, hot_in = sem("both_in"), sem("val_in"), sem("hot_in")
        vals_in, hot_used = sem("vals_in"), sem("hot_used")
        zeros_in = sem("zeros_in")

        with nc.Block() as block:
            @block.gpsimd
            def _(pool):
                pool.memset(tri, 1.0).then_inc(rconst, 1)
                pool.memset(ones16, 1.0).then_inc(rconst, 1)
                pool.memset(sm["one"], 1.0).then_inc(rconst, 1)
                pool.iota(sm["order"], pattern=[[-1, E]], base=E, channel_multiplier=0,
                          allow_small_or_imprecise_dtypes=True).then_inc(rconst, 1)
                pool.iota(pos_iota, pattern=[[1, P]], base=0, channel_multiplier=0,
                          allow_small_or_imprecise_dtypes=True).then_inc(rconst, 1)
                pool.iota(blk_iota, pattern=[[1, NB]], base=0, channel_multiplier=0,
                          allow_small_or_imprecise_dtypes=True).then_inc(rconst, 1)
                pool.iota(jiota, pattern=[[1, NG]], base=0, channel_multiplier=0,
                          allow_small_or_imprecise_dtypes=True).then_inc(rconst, 1)
                pool.iota(sm["pcol"], pattern=[[0, 1]], base=0, channel_multiplier=1,
                          allow_small_or_imprecise_dtypes=True).then_inc(rconst, 1)
                pool.iota(sm["tok"], pattern=[[P, NT]], base=-TOK, channel_multiplier=1,
                          allow_small_or_imprecise_dtypes=True).then_inc(rconst, 1)
                pool.wait_ge(rconst, 9)
                pool.affine_select(out=tri, in_=tri, compare_op=ALU.is_gt, fill=0.0, base=0,
                                   pattern=[[1, P]], channel_multiplier=-1).then_inc(rconst, 1)
                val = sm["val"].rearrange("p t c v -> p (t c) v")
                pool.wait_ge(val_in, 1)
                with pool.Fori(0, NT * TOPK // CH // 2) as i:
                    for m in range(2):
                        cols = DS(i * (2 * CH) + m * CH, CH)
                        pool.wait_ge(hot_used, 2 * i + m + 1)
                        pool.wait_ge(hot_in, 2 * i + m + 1)
                        pool.tensor_tensor(blk_vals[m], onehot_blk[m].unsqueeze(2).to_broadcast([P, CH, 2, NB]),
                                           val[:, cols, :].unsqueeze(3).to_broadcast([P, CH, 2, NB]),
                                           ALU.mult).then_inc(vals_in, 1)

            @block.scalar
            def _(act):
                act.wait_ge(gate_exp, 1)
                act.activation(sm["ed"], sm["dn"], ACT.Exp).then_inc(gate_exp, 1)

            @block.tensor
            def _(pe):
                pe.wait_ge(rconst, 10)
                pe.sem_inc(hot_used, 2)
                pe.wait_ge(both_in, 1)
                flat = both.rearrange("p t e -> p (t e)")
                pe.matmul(bank[0][:, 0:TE], tri, flat, start=True, stop=True)
                pe.matmul(bank[1][:, 0:TE], ones16, flat, start=True, stop=True).then_inc(counted, 1)
                pe.wait_ge(zeros_in, 1)
                pe.matmul(bank[2][:, 0:2 * NB], zeros[:, 0:P], zeros, start=True, stop=False, skip_group_check=True)
                with pe.Fori(0, NT * TOPK // CH // 2) as i:
                    for m in range(2):
                        pe.wait_ge(vals_in, 2 * i + m + 1)
                        for c in range(CH):
                            ins = pe.matmul(bank[2][:, 0:2 * NB], onehot_pos[m][:, c, :],
                                            blk_vals[m][:, c, :, :].rearrange("p v n -> p (v n)"),
                                            start=False, stop=False, skip_group_check=True)
                        ins.then_inc(hot_used, 1)
                pe.matmul(bank[2][:, 0:2 * NB], zeros[:, 0:P], zeros, start=False, stop=True,
                          skip_group_check=True).then_inc(mapped, 1)

            @block.vector
            def _(dve):
                done = [0]

                def then(ins):
                    done[0] += 1
                    ins.then_inc(routed, 1)
                    dve.wait_ge(routed, done[0])

                def per_token(ap):
                    return ap.unsqueeze(2).to_broadcast([P, NT, E])

                def per_expert(ap):
                    return ap.unsqueeze(1).to_broadcast([P, NT, E])

                def pick(src, top, onehot):
                    then(dve.tensor_reduce(top, src, AX, ALU.max))
                    then(dve.tensor_tensor(eq, src, per_token(top), ALU.is_equal))
                    then(dve.tensor_tensor(eq, eq, per_expert(sm["order"]), ALU.mult))
                    then(dve.tensor_reduce(sm["pm"], eq, AX, ALU.max))
                    then(dve.tensor_tensor(onehot, eq, per_token(sm["pm"]), ALU.is_equal))

                dve.memset(zeros, 0.0).then_inc(zeros_in, 1)
                dve.wait_ge(rconst, 10)
                pick(scr, sm["m1"], oh1)
                then(dve.scalar_tensor_tensor(out=rest, in0=oh1, scalar=-BIG, in1=scr, op0=ALU.mult, op1=ALU.add))
                pick(rest, sm["m2"], oh2)
                dve.tensor_tensor(both, oh1, oh2, ALU.add).then_inc(both_in, 1)
                dve.tensor_tensor(sm["dn"], sm["m2"], sm["m1"], ALU.subtract).then_inc(gate_exp, 1)
                dve.wait_ge(gate_exp, 2)
                then(dve.tensor_scalar(sm["m1"], sm["ed"], 1.0, None, ALU.add))
                gate = sm["val"][:, :, :, 1]
                then(dve.reciprocal(gate[:, :, 0], sm["m1"]))
                dve.tensor_tensor(gate[:, :, 1], sm["ed"], gate[:, :, 0], ALU.mult)
                dve.tensor_copy(sm["val"][:, :, :, 0], sm["tok"].unsqueeze(2).to_broadcast([P, NT, TOPK])).then_inc(val_in, 1)
                dve.wait_ge(counted, 1)
                then(dve.tensor_copy(tot, bank[1][:, 0:TE].rearrange("p (t e) -> p e t", e=E)))
                for e in range(E):
                    last = dve.tensor_tensor_scan(incl[:, e, :], sm["one"], tot[:, e, :], 0.0, ALU.mult, ALU.add)
                then(last)
                then(dve.tensor_tensor(excl, incl, tot, ALU.subtract))
                then(dve.tensor_tensor(rank, bank[0][:, 0:TE].rearrange("p (t e) -> p t e", e=E),
                                       excl.rearrange("p e t -> p t e"), ALU.add))
                then(dve.tensor_scalar(nbi, incl[:, :, NT - 1], float(G - 1), None, ALU.add))
                then(dve.tensor_scalar(nbi, nbi, 8, None, ALU.arith_shift_right))
                then(dve.tensor_copy(nbk, nbi))
                then(dve.tensor_tensor_scan(incb, sm["one"][:, 0:E], nbk, 0.0, ALU.mult, ALU.add))
                then(dve.tensor_tensor(offb, incb, nbk, ALU.subtract))
                then(dve.tensor_scalar(offb, offb, float(G // P), None, ALU.mult))
                for c, onehot in enumerate((oh1, oh2)):
                    then(dve.tensor_tensor(prod, onehot, rank, ALU.mult))
                    then(dve.tensor_reduce(sm["rk"][:, :, c], prod, AX, ALU.add))
                    then(dve.tensor_tensor(prod, onehot, per_expert(offb), ALU.mult))
                    then(dve.tensor_reduce(sm["obk"][:, :, c], prod, AX, ALU.add))
                then(dve.tensor_copy(sm["ri"], sm["rk"]))
                then(dve.tensor_scalar(sm["rp"], sm["ri"], P - 1, None, ALU.bitwise_and))
                then(dve.tensor_copy(sm["pos"], sm["rp"].rearrange("p t c -> p (t c)")))
                then(dve.tensor_scalar(sm["rp"], sm["ri"], 7, None, ALU.arith_shift_right))
                then(dve.tensor_copy(sm["blk"], sm["rp"].rearrange("p t c -> p (t c)")))
                then(dve.tensor_tensor(sm["blk"], sm["blk"], sm["obk"].rearrange("p t c -> p (t c)"), ALU.add))
                then(dve.tensor_tensor(cmp, incb.unsqueeze(1).to_broadcast([P, NG, E]),
                                       jiota.unsqueeze(2).to_broadcast([P, NG, E]), ALU.is_le))
                then(dve.tensor_reduce(ta[:, 0:NG], cmp, AX, ALU.add))
                then(dve.tensor_scalar(expert_of, ta[:, 0:NG], float(E - 1), None, ALU.min))
                with dve.Fori(0, NT * TOPK // CH // 2) as i:
                    for m in range(2):
                        cols = DS(i * (2 * CH) + m * CH, CH)
                        dve.wait_ge(hot_used, 2 * i + m + 1)
                        dve.tensor_tensor(onehot_blk[m], blk_iota.unsqueeze(1).to_broadcast([P, CH, NB]),
                                          sm["blk"][:, cols].unsqueeze(2).to_broadcast([P, CH, NB]), ALU.is_equal)
                        dve.tensor_tensor(onehot_pos[m], pos_iota.unsqueeze(1).to_broadcast([P, CH, P]),
                                          sm["pos"][:, cols].unsqueeze(2).to_broadcast([P, CH, P]),
                                          ALU.is_equal).then_inc(hot_in, 1)
                dve.wait_ge(mapped, 1)
                table = bank[2][:, 0:2 * NB].rearrange("p (v n) -> p v n", v=2)
                dve.tensor_copy(slot_gate, table[:, 1, :])
                then(dve.tensor_scalar(tb, table[:, 0, :], 0.0, sm["pcol"], ALU.is_equal, ALU.mult))
                then(dve.scalar_tensor_tensor(out=slot_row, in0=table[:, 0, :], scalar=float(TOK), in1=tb,
                                              op0=ALU.add, op1=ALU.add))


        H = G // P
        FQ = FC // 4
        bX, bH, bY = bank[0], bank[1:5], bank[5:7]
        xg = [[xin[0], xin[1]], [xb[0], xb[1]]]
        yg = [[res[0], res[1]], [attn[0], attn[1]]]
        xh = [view(stage[0], m * D, KC, G, dt=F16) for m in range(2)]
        xl = [view(stage[0], (2 + m) * D, KC, G, dt=F16) for m in range(2)]
        hid = [view(buf, q * FQ * G, FQ * G) for buf in (ss, small) for q in range(2)]
        hh, hl = view(pt, 0, FC, G, dt=F16), view(spare[0], 0, FC, G, dt=F16)
        names = ("xgt xgh_in xgl_in h0 h1 h2 h3 hid0 hid1 hid2 hid3 hh0 hh1 hh2 hh3 hl0 hl1 hl2 hl3 "
                 "y_ps0 y_ps1 y_in0 y_in1 from_in to_in").split()
        e = {n: sem("e_" + n) for n in names}
        gathered = [sem(f"gathered{m}") for m in range(2)]
        scattered = [sem(f"scattered{m}") for m in range(2)]

        def groups(run, emit, first=0):
            for j in range(first):
                emit(j // 2, j % 2)
            with run.Fori(first // 2, (NG - 3) // 2) as i:
                for m in range(2):
                    emit(i, m)
            for j in range(NG - 3, NG):
                emit(j // 2, j % 2)

        def upto(i, m, ahead=0):
            return 2 * i + (m + ahead + 3)

        def slot(i, m, ahead):
            return (m + ahead) % 2, i + (m + ahead) // 2

        def beyond(i, m, ahead):
            return isinstance(i, int) and 2 * i + m + ahead >= NG

        def quarter(ap, q):
            return ap[:, q * FQ:(q + 1) * FQ, :].rearrange("p f n -> p (f n)")

        with nc.Block() as block:
            @block.gpsimd
            def _(pool):
                wait_rows = stepper(pool, "rows_value", 1)
                wait_y = [stepper(pool, f"y{h}_value", 3) for h in range(H)]

                def gather(i, m, ahead):
                    if beyond(i, m, ahead):
                        return
                    n, _k = slot(i, m, ahead)
                    pool.wait_ge(e["from_in"], upto(i, m, ahead))
                    wait_rows(e["xgt"])
                    for h in range(H):
                        pool.indirect_dma_start(out=xg[n][h][:], out_offset=None, in_=xn_rows,
                                                in_offset=bass.IndirectOffsetOnAxis(ap=rows_from[n][:, h:h + 1], axis=0))\
                            .then_inc(gathered[n], 16)

                def step(i, m):
                    gather(i, m, 3)
                    n, k = slot(i, m, -1)
                    pool.wait_ge(e["to_in"], upto(i, m))
                    for h in range(H):
                        if h:
                            pool.wait_ge(scattered[m], 16 * (H * i + h))
                        elif not (isinstance(k, int) and k < 0):
                            pool.wait_ge(scattered[n], 16 * (H * k + H))
                        wait_y[h](e[f"y_in{h}"])
                        pool.indirect_dma_start(out=out, in_=yg[m][h][:], in_offset=None, compute_op=ALU.add,
                                                out_offset=bass.IndirectOffsetOnAxis(ap=rows_to[m][:, h:h + 1], axis=0))\
                            .then_inc(scattered[m], 16)

                for n in range(3):
                    gather(0, n, 0)
                groups(pool, step, first=2)
                for m in range(2):
                    pool.wait_ge(scattered[m], 16 * H * ((NG + 1 - m) // 2))

            @block.tensor
            def _(pe):
                for n in ("xgt", "h0", "h1", "h2", "h3", "y_ps0", "y_ps1"):
                    pe.sem_inc(e[n], 2)

                def turn_rows(i, m, ahead):
                    if beyond(i, m, ahead):
                        return
                    n, k = slot(i, m, ahead)
                    pe.wait_ge(gathered[n], 16 * (H * k + H))
                    pe.wait_ge(e["xgl_in"], upto(i, m, ahead - 1))
                    for h in range(H):
                        for c in range(KC):
                            c0 = c * G + h * P
                            ins = pe.transpose(bX[:, c0:c0 + P], xg[n][h][:, c * P:(c + 1) * P], ident[:])
                    ins.then_inc(e["xgt"], 1)

                def first(i, m, ahead):
                    if beyond(i, m, ahead):
                        return
                    n, k = slot(i, m, ahead)
                    which = pe.value_load(expert_of[0:1, DS(2 * i + m + ahead, 1)], min_val=0, max_val=E - 1)
                    pe.wait_ge(e["xgl_in"], upto(i, m, ahead))
                    xt = (xh[n], xl[n])
                    for f in range(FC):
                        if f % FQ == 0:
                            pe.wait_ge(e[f"hid{f // FQ}"], upto(i, m, ahead - 1))
                        ins = three(pe, bH[f // FQ][:, f % FQ * G:(f % FQ + 1) * G],
                                    lambda a, c: (w1h, w1l)[a][:, DS(which * (KC * F) + (c * F + f * P), P)],
                                    lambda a, c: xt[a][:, c, :], range(KC))
                        if f % FQ == FQ - 1:
                            ins.then_inc(e[f"h{f // FQ}"], 1)

                def step(i, m):
                    first(i, m, 1)
                    turn_rows(i, m, 2)
                    which = pe.value_load(expert_of[0:1, DS(2 * i + m, 1)], min_val=0, max_val=E - 1)
                    for h in range(H):
                        pe.wait_ge(e[f"y_in{h}"], upto(i, m, -1))
                        for f in range(FC):
                            if h == 0 and f % FQ == 0:
                                pe.wait_ge(e[f"hl{f // FQ}"], upto(i, m))
                            for a, c in ((0, 0), (0, 1), (1, 0)):
                                ins = pe.matmul(bY[h][:, 0:D], (hh, hl)[a][:, f, h * P:(h + 1) * P],
                                                (w2h, w2l)[c][:, DS(which * (FC * D) + f * D, D)],
                                                start=(f == a == c == 0), stop=(f == FC - 1 and a == 1))
                        ins.then_inc(e[f"y_ps{h}"], 1)

                turn_rows(0, 0, 0)
                first(0, 0, 0)
                turn_rows(0, 1, 0)
                groups(pe, step)

            @block.scalar
            def _(act):
                for n in ("xgh_in", "hid0", "hid1", "hid2", "hid3", "hh0", "hh1", "hh2", "hh3"):
                    act.sem_inc(e[n], 2)

                def rows_hi(i, m, ahead):
                    if beyond(i, m, ahead):
                        return
                    n, _k = slot(i, m, ahead)
                    act.wait_ge(e["xgt"], upto(i, m, ahead))
                    act.wait_ge(e["h3"], upto(i, m, ahead - 2))
                    act.activation(xh[n].rearrange("p k n -> p (k n)"), bX[:], ACT.Copy,
                                   scale=XS).then_inc(e["xgh_in"], 1)

                def gelu(i, m, ahead):
                    if beyond(i, m, ahead):
                        return
                    for q in range(4):
                        act.wait_ge(e[f"h{q}"], upto(i, m, ahead))
                        act.wait_ge(e[f"hl{q}"], upto(i, m, ahead - 1))
                        act.activation(hid[q], bH[q][:], ACT.Gelu, scale=UN_XW).then_inc(e[f"hid{q}"], 1)

                def step(i, m):
                    act.wait_ge(e["y_ps1"], upto(i, m, -1))
                    for q in range(4):
                        act.wait_ge(e[f"hid{q}"], upto(i, m))
                        act.activation(quarter(hh, q), hid[q], ACT.Copy, scale=HS).then_inc(e[f"hh{q}"], 1)
                    gelu(i, m, 1)
                    rows_hi(i, m, 2)

                rows_hi(0, 0, 0)
                rows_hi(0, 1, 0)
                gelu(0, 0, 0)
                groups(act, step)

            @block.vector
            def _(dve):
                for n in ("xgl_in", "hl0", "hl1", "hl2", "hl3", "y_in0", "y_in1", "from_in", "to_in"):
                    dve.sem_inc(e[n], 2)

                def rows_of(i, m, ahead):
                    if beyond(i, m, ahead):
                        return
                    n, k = slot(i, m, ahead)
                    if not (isinstance(k, int) and k == 0):
                        dve.wait_ge(gathered[n], 16 * H * k)
                    dve.tensor_copy(rows_from[n][:], slot_row[:, DS(4 * i + H * (m + ahead), H)]).then_inc(e["from_in"], 1)

                def rows_lo(i, m, ahead):
                    if beyond(i, m, ahead):
                        return
                    n, _k = slot(i, m, ahead)
                    dve.wait_ge(e["xgh_in"], upto(i, m, ahead))
                    dve.scalar_tensor_tensor(out=xl[n].rearrange("p k n -> p (k n)"), in0=bX[:], scalar=XS,
                                             in1=xh[n].rearrange("p k n -> p (k n)"),
                                             op0=ALU.mult, op1=ALU.subtract).then_inc(e["xgl_in"], 1)

                def step(i, m):
                    for q in range(4):
                        dve.wait_ge(e[f"hh{q}"], upto(i, m))
                        dve.scalar_tensor_tensor(out=quarter(hl, q), in0=hid[q], scalar=HS, in1=quarter(hh, q),
                                                 op0=ALU.mult, op1=ALU.subtract).then_inc(e[f"hl{q}"], 1)
                    rows_of(i, m, 3)
                    if not (isinstance(i, int) and i == 0):
                        dve.wait_ge(scattered[m], 16 * H * i)
                    dve.tensor_copy(rows_to[m][:], slot_row[:, DS(4 * i + H * m, H)]).then_inc(e["to_in"], 1)
                    rows_lo(i, m, 2)
                    for h in range(H):
                        dve.wait_ge(e[f"y_ps{h}"], upto(i, m))
                        dve.tensor_scalar(yg[m][h][:], bY[h][:, 0:D], slot_gate[:, DS(4 * i + (H * m + h), 1)], UN_HW,
                                          ALU.mult, ALU.mult).then_inc(e[f"y_in{h}"], 1)

                for n in range(3):
                    rows_of(0, n, 0)
                rows_lo(0, 0, 0)
                rows_lo(0, 1, 0)
                groups(dve, step, first=2)


def kernel(**inputs):
    import numpy as _np
    import concourse.bacc as _bacc
    from concourse import mybir as _mybir
    from concourse.bass_utils import run_bass_kernel_spmd as _run

    a = {n: _np.asarray(v) for n, v in inputs.items()}
    w1 = a["L0_ffn_expert_w1"].transpose(0, 2, 1)
    w2 = a["L0_ffn_expert_w2"].transpose(0, 2, 1)
    w2 = w2.reshape(E, 2, FC // 2, P, D).transpose(0, 1, 3, 2, 4)
    arrays = {
        "x": a["L0_attn_x"].reshape(TOK, D),
        "wq": a["L0_attn_Wq"], "wk": a["L0_attn_Wk"], "wv": a["L0_attn_Wv"], "wo": a["L0_attn_Wo"],
        "bo": a["L0_attn_bo"],
        "rwt": a["L0_ffn_router_w"].T,
        "w1c": w1.reshape(E * KC * P, F),
        "w2c": w2.reshape(E * 2 * P, FC // 2 * D),
    }
    arrays = {n: _np.ascontiguousarray(v) for n, v in arrays.items()}
    nc = _bacc.Bacc("TRN2", target_bir_lowering=False, num_devices=1)
    args = [nc.dram_tensor(n, v.shape, _mybir.dt.from_np(v.dtype), kind="ExternalInput").ap()
            for n, v in arrays.items()]
    out = nc.dram_tensor("out", (TOK + PAD, D), F32, kind="ExternalOutput").ap()
    block_kernel(nc, *args, out)
    got = _run(nc, [arrays], core_ids=[0]).results[0]["out"]
    return got[:TOK].reshape(B, SEQ, D)
```

```python
from contextlib import ExitStack

import concourse.bass as bass
from concourse import mybir

ALU = mybir.AluOpType
ACT = mybir.ActivationFunctionType
F32 = mybir.dt.float32
F16 = mybir.dt.float16
I32 = mybir.dt.int32
AX = mybir.AxisListType.X

P = 128
B, SEQ, D = 2, 2048, 256
TOK = B * SEQ
NT = TOK // P
NW = SEQ // P
HEADS, LH, DH = 16, 4, 16
GD = (HEADS - LH) * DH
LD = LH * DH
KC = D // P
E, F, TOPK = 8, 1024, 2
FC = F // P
G = 2 * P
NG = (TOK * TOPK + E * (G - 1)) // G
NB = G // P * NG
PAD = P
BIG = 3.0e38
XS, WS, HS, AS = 256.0, 64.0, 16.0, 64.0
QS = 16.0
UN_XW, UN_AW, UN_HW = 1 / (XS * WS), 1 / (AS * WS), 1 / (HS * WS)
CQ, CK, CR, CV = 0, GD, 2 * GD, 2 * GD + E
NTOKC = CV + D
GA, GB = 128, 64
CTX = GA + 1 + GB + 1
VC = LD + CTX
DS = bass.ds


def block_kernel(nc, x, wq, wk, wv, wo, bo, rwt, w1c, w2c, out):
    with ExitStack() as ctx:
        def sb(name, shape, dt=F32):
            return ctx.enter_context(nc.sbuf_tensor(name, shape, dt))

        def sem(name):
            return ctx.enter_context(nc.semaphore(name))

        def pair(name, shape, dt=F32):
            return [sb(f"{name}{b}", shape, dt) for b in range(2)]

        xn_rows = nc.dram_tensor("xn_rows", (TOK + PAD, D), F32).ap()

        w1h, w1l = sb("w1h", [P, E * KC * F], F16), sb("w1l", [P, E * KC * F], F16)
        w2h, w2l = sb("w2h", [P, E * FC * D], F16), sb("w2l", [P, E * FC * D], F16)
        stage = pair("stage", [P, F])
        wtok = [sb(f"wtok{n}", [P, KC, NTOKC], F16) for n in "hl"]
        wqk = [sb(f"wqk{n}", [P, KC, 2, LH, 2, DH], F16) for n in "hl"]
        wout = [sb(f"wout{n}", [P, KC, D], F16) for n in "hl"]
        ident = sb("ident", [P, P])
        causal = sb("causal", [P, 3 * P])
        ctx_mask = sb("ctx_mask", [P, CTX])
        bias = sb("bias", [P, D])
        minus_half = sb("minus_half", [P, 1])
        scores = sb("scores", [P, NT, E])

        xin, xn, xb = pair("xin", [P, D]), pair("xn", [P, D]), pair("xb", [P, D])
        stats, mv = pair("stats", [P, 6]), pair("mv", [P, 2])
        veps, rstd = pair("veps", [P, 1]), pair("rstd", [P, 1])
        xth, xtl = pair("xth", [P, D], F16), pair("xtl", [P, D], F16)
        low_row = sb("low_row", [P, LH + 1])
        qm, qt, kt = pair("qm", [P, P], F16), pair("qt", [P, P], F16), pair("kt", [P, 2, 2 * P], F16)
        val = [pair(f"val{b}_", [P, VC]) for b in range(2)]
        qmax, qsum, qrec = pair("qmax", [P, 12]), pair("qsum", [P, 12]), pair("qrec", [P, 12])
        qs, krelu, ke = pair("qs", [P, D]), pair("krelu", [P, GD]), pair("ke", [P, D])
        ss, pt = sb("ss", [P, LH, 2 * P]), sb("pt", [P, LH, 2, P])
        spare = pair("spare", [P, LH, 2 * P])
        negmax, rsum, rrec = pair("negmax", [P, LH]), pair("rsum", [P, LH]), pair("rrec", [P, LH])
        cum, cum0 = pair("cum", [P, CTX]), pair("cum0", [P, CTX])
        new0, new1 = pair("new0", [P, CTX]), pair("new1", [P, CTX])
        den, rden = pair("den", [P, 2, 2]), pair("rden", [P, 2, 2])
        qgt = pair("qgt", [P, 2, P])
        attn, res = pair("attn", [P, D]), pair("res", [P, D])
        rows_from, rows_to = pair("rows_from", [P, 2], I32), pair("rows_to", [P, 2], I32)
        ath, atl = pair("ath", [P, D], F16), pair("atl", [P, D], F16)

        bank = [ctx.enter_context(nc.psum_tensor(f"bank{n}", [P, 512], F32)) for n in range(8)]

        def view(t, off, *shape, dt=F32):
            n = 1
            for m in shape:
                n *= m
            flat = t[:].rearrange("p a b -> p (a b)") if len(t.shape) == 3 else (
                t[:].rearrange("p a b c -> p (a b c)") if len(t.shape) == 4 else t[:])
            if dt is F16:
                ap = flat[:, off:off + n // 2].bitcast(F16)
            else:
                ap = flat[:, off:off + n]
                if dt is not F32:
                    ap = ap.bitcast(dt)
            names = "abcd"[:len(shape)]
            if len(shape) == 1:
                return ap
            return ap.rearrange(f"p ({' '.join(names)}) -> p {' '.join(names)}",
                                **{c: m for c, m in zip(names[:-1], shape[:-1])})

        small = spare[1]
        c0 = 0
        sm = {}
        for name, shape, dt in (("m1", (NT,), F32), ("m2", (NT,), F32), ("pm", (NT,), F32), ("ed", (NT,), F32),
                                ("dn", (NT,), F32), ("val", (NT, TOPK, 2), F32), ("rk", (NT, TOPK), F32),
                                ("ri", (NT, TOPK), I32), ("rp", (NT, TOPK), I32),
                                ("pos", (NT * TOPK,), F32), ("blk", (NT * TOPK,), F32), ("order", (E,), F32),
                                ("one", (NT,), F32), ("pcol", (1,), F32), ("tok", (NT,), F32), ("jiota", (NG,), F32)):
            n = 1
            for m in shape:
                n *= m
            sm[name] = view(small, c0, *shape, dt=dt)
            c0 += n if dt is not F16 else (n + 1) // 2

        got_w, got_c = sem("got_w"), sem("got_c")
        pool_const, zeroed, padded = sem("pool_const"), sem("zeroed"), sem("padded")
        w_hi, w_lo = sem("w_hi"), sem("w_lo")

        names = ("stats_in aggregated veps_in rstd_in xn_in xb_in xnt xth_in xtl_in tok0 qk tok1 qm_in kh_in qt_in kt_in "
                 "v_in kneg_in kexp_in qmax_in qsub_in qexp_in tok0_read qsum_in qrec_in qn_in ke_in qgt_ps "
                 "head0 head1 head2 head3 negmax0 negmax1 prob0 prob1 pt_ps pta_in ptb_in ctx_ps new0_in new_in "
                 "cum0_in den_in rden_in qgt_in att_ps rrec_in lin_in attn_in cum_in at_ps ath_in atl_in pr_ps res_in "
                 "stage_up stage_hi stage_lo").split()
        opened = sem("opened")
        s = {n: sem(n) for n in names}
        x_loaded = [sem(f"x_loaded{b}") for b in range(2)]
        xn_stored = [sem(f"xn_stored{b}") for b in range(2)]
        res_stored = [sem(f"res_stored{b}") for b in range(2)]
        xb_loaded = [sem(f"xb_loaded{b}") for b in range(2)]
        w_loaded = [sem(f"w_loaded{b}") for b in range(2)]

        wsrc = {"q": ss[:, 0:2, :], "k": ss[:, 2:4, :], "v": spare[0][:, 0:2, :], "o": spare[0][:, 2:4, :]}
        rsrc = qs[0][:, 0:KC * E].rearrange("p (k e) -> p k e", k=KC)
        zero_rows = kt[0][:].rearrange("p a n -> p (a n)").bitcast(F32)

        jobs = [(lambda n: wtok[n][:, :, CQ:CQ + GD], wsrc["q"][:, :, LD:D]),
                (lambda n: wtok[n][:, :, CK:CK + GD], wsrc["k"][:, :, LD:D]),
                (lambda n: wtok[n][:, :, CR:CR + E], rsrc),
                (lambda n: wtok[n][:, :, CV:CV + D], wsrc["v"]),
                (lambda n: wout[n][:], wsrc["o"])]
        for k in range(KC):
            for m, name in enumerate("qk"):
                for c in range(2):
                    jobs.append((lambda n, k=k, m=m, c=c: wqk[n][:, k, m, :, c, :],
                                 wsrc[name][:, k, 0:LD].rearrange("p (h e) -> p h e", e=DH)))

        with nc.Block() as block:
            @block.sync
            def _(sp):
                for b in range(2):
                    sp.dma_start(xin[b][:], x[b * SEQ:b * SEQ + P, :]).then_inc(x_loaded[b], 16)
                for name, w in (("q", wq), ("k", wk), ("v", wv), ("o", wo)):
                    sp.dma_start(wsrc[name], w.rearrange("(k p) n -> p k n", p=P)).then_inc(got_w, 16)
                sp.dma_start(rsrc, rwt.rearrange("(k p) n -> p k n", p=P)).then_inc(got_w, 16)
                sp.dma_start(bias[:], bo.partition_broadcast(P)).then_inc(got_c, 16)
                for m, w in enumerate((w1c, w2c)):
                    sp.dma_start(stage[m][:], w[0:P, :]).then_inc(w_loaded[m], 16)
                sp.wait_ge(zeroed, 1)
                sp.dma_start(xn_rows[TOK:TOK + PAD, :], zero_rows).then_inc(padded, 16)
                sp.dma_start(out[TOK:TOK + PAD, :], zero_rows).then_inc(padded, 16)
                sp.wait_ge(got_c, 16)
                sp.wait_ge(padded, 32)

            @block.gpsimd
            def _(pool):
                pool.memset(ident[:], 0.0).then_inc(pool_const, 1)
                pool.memset(causal[:, 0:2 * P], 0.0).then_inc(pool_const, 1)
                pool.memset(causal[:, 2 * P:3 * P], BIG).then_inc(pool_const, 1)
                pool.memset(ctx_mask[:], 1.0).then_inc(pool_const, 1)
                pool.memset(minus_half[:], -0.5).then_inc(pool_const, 1)
                pool.memset(low_row[:], -QS * UN_XW).then_inc(pool_const, 1)
                pool.wait_ge(pool_const, 6)
                pool.affine_select(out=ident[:], in_=ident[:], compare_op=ALU.not_equal, fill=1.0, base=0,
                                   pattern=[[-1, P]], channel_multiplier=1).then_inc(pool_const, 1)
                pool.affine_select(out=causal[:, P:2 * P], in_=causal[:, P:2 * P], compare_op=ALU.is_ge,
                                   fill=BIG, base=0, pattern=[[-1, P]], channel_multiplier=1).then_inc(pool_const, 1)
                step = 8
                for c0, width in ((0, GA), (GA + 1, GB)):
                    v = ctx_mask[:, c0:c0 + width].rearrange("p (h e) -> p h e", e=DH)
                    for base, mult, sign in ((0, 1, -DH), (DH - 1, -1, DH)):
                        pool.wait_ge(pool_const, step)
                        pool.affine_select(out=v, in_=v, compare_op=ALU.is_ge, fill=0.0, base=base,
                                           pattern=[[sign, width // DH], [0, DH]],
                                           channel_multiplier=mult).then_inc(pool_const, 1)
                        step += 1
                for base, mult, sign in ((-DH, 1, -32), (31, -1, 32)):
                    pool.wait_ge(pool_const, step)
                    pool.affine_select(out=low_row[:, 0:LH], in_=low_row[:, 0:LH], compare_op=ALU.is_ge, fill=0.0,
                                       base=base, pattern=[[sign, LH]], channel_multiplier=mult).then_inc(pool_const, 1)
                    step += 1
                pool.memset(sm["one"], 1.0)
                for name, pattern, base, mult in (("order", [-1, E], E, 0), ("jiota", [1, NG], 0, 0),
                                                  ("pcol", [0, 1], 0, 1), ("tok", [P, NT], -TOK, 1)):
                    ins = pool.iota(sm[name], pattern=[pattern], base=base, channel_multiplier=mult,
                                    allow_small_or_imprecise_dtypes=True)
                ins.then_inc(pool_const, 1)
                pool.wait_ge(s["veps_in"], 1)
                pool.tensor_tensor(rstd[0][:], veps[0][:], minus_half[:], ALU.pow).then_inc(s["rstd_in"], 1)

            @block.scalar
            def _(act):
                act.wait_ge(got_w, 80)
                for dst, src in jobs:
                    act.activation(dst(0), src, ACT.Copy, scale=WS).then_inc(w_hi, 1)

            @block.vector
            def _(dve):
                for b in range(2):
                    dve.memset(kt[b][:], 0.0).then_inc(zeroed, 1)
                    dve.memset(val[b][1][:, 0:LD], 0.0)
                    dve.memset(cum[b][:], 0.0)
                    dve.memset(ke[b][:, GD:D], 0.0)
                    for odd in range(2):
                        dve.memset(val[b][odd][:, LD + GA:LD + GA + 1], 1.0)
                        dve.memset(val[b][odd][:, VC - 1:VC], 1.0)
                dve.wait_ge(x_loaded[0], 16)
                dve.bn_stats(stats[0][:], xin[0][:]).then_inc(s["stats_in"], 1)
                dve.wait_ge(s["stats_in"], 1)
                dve.bn_aggr(mv[0][:], stats[0][:]).then_inc(s["aggregated"], 1)
                dve.wait_ge(s["aggregated"], 1)
                dve.tensor_scalar(veps[0][:], mv[0][:, 1:2], 1e-5, None, ALU.add).then_inc(s["veps_in"], 1)
                dve.wait_ge(s["rstd_in"], 1)
                dve.tensor_scalar(xn[0][:], xin[0][:], mv[0][:, 0:1], rstd[0][:], ALU.subtract,
                                  ALU.mult).then_inc(s["xn_in"], 1)
                for c, (dst, src) in enumerate(jobs):
                    dve.wait_ge(w_hi, c + 1)
                    dve.scalar_tensor_tensor(out=dst(1), in0=src, scalar=WS, in1=dst(0),
                                             op0=ALU.mult, op1=ALU.subtract).then_inc(w_lo, 1)
                dve.wait_ge(pool_const, 14)
                dve.tensor_reduce(low_row[:, LH:LH + 1], low_row[:, 0:LH], AX, ALU.add)
                dve.wait_ge(w_lo, len(jobs))
                for b in range(2):
                    dve.memset(qs[b][:, GD:D], 0.0)

        def stepper(eng, name, first):
            value = eng.alloc_register(name)
            eng.reg_mov(value, first)

            def wait(semaphore, written_out=None):
                if written_out is not None:
                    eng.wait_ge(semaphore, written_out)
                else:
                    eng.wait_ge(semaphore, value)
                    eng.reg_add(value, value, 1)
            return wait

        class Step:

            def __init__(self, eng, i, b, u=None):
                self.eng, self.i, self.b, self.u = eng, i, b, i % 2 if u is None else u

            def has(self, off):
                return not isinstance(self.i, int) or 0 <= 2 * self.i + self.b + off < NT

            def last(self, n):
                return isinstance(self.i, int) and 2 * self.i + self.b == NT + n

            def row(self, off):
                return (self.b + off) % 2

            def window(self, off):
                return self.i + (self.b + off) // 2

            def odd(self, off):
                return (self.u + (self.b + off) // 2) % 2

            def own(self, off):
                return slice(self.odd(off) * P, (self.odd(off) + 1) * P)

            def first_row(self, off):
                return (self.row(off) * NW + self.window(off)) * P

            def wait(self, semaphore, off):
                c = self.b + off + 1
                if isinstance(self.i, int):
                    if 2 * self.i + c > 0:
                        self.eng.wait_ge(semaphore, 2 * self.i + c)
                else:
                    self.eng.wait_ge(semaphore, 2 * self.i + c)

            def wait_dma(self, semaphores, off):
                k = self.window(off) + 1
                if not isinstance(k, int) or k > 0:
                    self.eng.wait_ge(semaphores[self.row(off)], 16 * k)

        HEAD = 4

        def tile_stepper(eng, name, off):
            wait = stepper(eng, name, HEAD + off + 1)
            return lambda semaphore, t: wait(semaphore, 2 * t.i + t.b + off + 1 if isinstance(t.i, int) else None)

        def steps(eng, emit):
            for t in range(HEAD):
                emit(Step(eng, t // 2, t % 2))
            with eng.Fori(HEAD // 4, (NT - 4) // 4) as n:
                for t in range(4):
                    emit(Step(eng, 2 * n + t // 2, t % 2, t // 2))
            for t in range(NT - 4, NT + 3):
                emit(Step(eng, t // 2, t % 2))

        def three(pe, dst, lhs, rhs, chunks):
            terms = [(k, a, c) for k in chunks for a, c in ((0, 0), (0, 1), (1, 0))]
            for n, (k, a, c) in enumerate(terms):
                ins = pe.matmul(dst, lhs(a, k), rhs(c, k), start=(n == 0), stop=(n == len(terms) - 1))
            return ins

        b_xnt, b_tok0, b_tok1, b_s, b_ctx, b_att, b_out = bank[0], bank[1], bank[2], bank[3:5], bank[5], bank[6], bank[7]

        TE = NT * E
        eq, oh1, oh2, rest = (view(ss, c * TE, NT, E) for c in range(4))
        rank, prod = view(spare[0], 0, NT, E), view(spare[0], TE, NT, E)
        excl, tot = view(spare[0], 2 * TE, E, NT), view(spare[0], 3 * TE, E, NT)
        both = view(spare[0], TE, NT, E, dt=F16)
        incl = view(pt, TE, E, NT)
        tri, ones16 = view(pt, 2 * TE, P, dt=F16), view(pt, 2 * TE + P // 2, P, dt=F16)
        pos_iota, blk_iota = view(pt, 2 * TE + P, P), view(pt, 2 * TE + 2 * P, NB)
        nbk, nbi, incb, offb = view(xb[0], 0, E), view(xb[0], E, E, dt=I32), view(xb[0], 2 * E, E), view(xb[0], 3 * E, E)
        cmp = view(ss, 0, NG, E)
        CH, MB = 2, 4
        onehot_pos = [view(spare[0], m * CH * P, CH, P) for m in range(MB)]
        onehot_blk = [view(stage[m % 2], m // 2 * (3 * CH * NB), CH, NB) for m in range(MB)]
        blk_vals = [view(stage[m % 2], (3 * (m // 2) + 1) * CH * NB, CH, 2, NB) for m in range(MB)]
        slot_row = view(xn[0], 0, NB, dt=I32)
        slot_gate = view(xn[0], NB, NB)
        expert_of = view(xn[1], 0, NG, dt=I32)
        ta, tb = view(xn[1], NB, NB), view(xn[1], 2 * NB, NB)
        zeros = view(qgt[0], 0, 2 * NB, dt=F16)
        scr = scores[:]

        routed, rconst = sem("routed"), sem("rconst")
        gate_exp, counted, mapped = sem("gate_exp"), sem("counted"), sem("mapped")
        both_in, val_in, hot_in = sem("both_in"), sem("val_in"), sem("hot_in")
        vals_in, vals2_in, hot_used = sem("vals_in"), sem("vals2_in"), sem("hot_used")
        zeros_in = sem("zeros_in")

        def route_constants(pool):
            pool.wait_ge(s["att_ps"], NT)
            pool.memset(tri, 1.0).then_inc(rconst, 1)
            pool.memset(ones16, 1.0).then_inc(rconst, 1)
            pool.iota(pos_iota, pattern=[[1, P]], base=0, channel_multiplier=0,
                      allow_small_or_imprecise_dtypes=True).then_inc(rconst, 1)
            pool.iota(blk_iota, pattern=[[1, NB]], base=0, channel_multiplier=0,
                      allow_small_or_imprecise_dtypes=True).then_inc(rconst, 1)
            pool.wait_ge(rconst, 4)
            pool.affine_select(out=tri, in_=tri, compare_op=ALU.is_gt, fill=0.0, base=0,
                               pattern=[[1, P]], channel_multiplier=-1).then_inc(rconst, 1)

        def route_values(pool):
            val = sm["val"].rearrange("p t c v -> p (t c) v")
            pool.wait_ge(val_in, 1)
            with pool.Fori(0, NT * TOPK // CH // MB) as i:
                for m in range(MB):
                    col = DS(i * (MB * CH) + m * CH, 1)
                    pool.wait_ge(hot_used, MB * i + m + 1)
                    pool.wait_ge(hot_in, MB * i + m + 1)
                    pool.tensor_tensor(blk_vals[m][:, 0, :, :], onehot_blk[m][:, 0:1, :].to_broadcast([P, 2, NB]),
                                       val[:, col, :].rearrange("p c v -> p (c v)").unsqueeze(2)
                                       .to_broadcast([P, 2, NB]), ALU.mult).then_inc(vals_in, 1)

        def route_act(act):
            act.wait_ge(gate_exp, 1)
            act.activation(sm["ed"], sm["dn"], ACT.Exp).then_inc(gate_exp, 1)
            val = sm["val"].rearrange("p t c v -> p (t c) v")
            act.wait_ge(val_in, 1)
            with act.Fori(0, NT * TOPK // CH // MB) as i:
                for m in range(MB):
                    col = DS(i * (MB * CH) + m * CH + 1, 1)
                    act.wait_ge(hot_used, MB * i + m + 1)
                    act.wait_ge(hot_in, MB * i + m + 1)
                    for v in range(2):
                        ins = act.activation(blk_vals[m][:, 1, v, :], onehot_blk[m][:, 1, :], ACT.Copy,
                                             scale=val[:, col, v])
                    ins.then_inc(vals2_in, 1)

        def route_counts(pe):
            pe.wait_ge(rconst, 5)
            pe.sem_inc(hot_used, MB)
            pe.wait_ge(both_in, 1)
            flat = both.rearrange("p t e -> p (t e)")
            pe.matmul(bank[0][:, 0:TE], tri, flat, start=True, stop=True)
            pe.matmul(bank[1][:, 0:TE], ones16, flat, start=True, stop=True).then_inc(counted, 1)

        def route_tables(pe):
            pe.wait_ge(zeros_in, 1)
            pe.matmul(bank[2][:, 0:2 * NB], zeros[:, 0:P], zeros, start=True, stop=False, skip_group_check=True)
            with pe.Fori(0, NT * TOPK // CH // MB) as i:
                for m in range(MB):
                    pe.wait_ge(vals_in, MB * i + m + 1)
                    pe.wait_ge(vals2_in, MB * i + m + 1)
                    for c in range(CH):
                        ins = pe.matmul(bank[2][:, 0:2 * NB], onehot_pos[m][:, c, :],
                                        blk_vals[m][:, c, :, :].rearrange("p v n -> p (v n)"),
                                        start=False, stop=False, skip_group_check=True)
                    ins.then_inc(hot_used, 1)
            pe.matmul(bank[2][:, 0:2 * NB], zeros[:, 0:P], zeros, start=False, stop=True,
                      skip_group_check=True).then_inc(mapped, 1)

        done = [0]

        def then(dve, ins):
            done[0] += 1
            ins.then_inc(routed, 1)
            dve.wait_ge(routed, done[0])

        def per_token(ap):
            return ap.unsqueeze(2).to_broadcast([P, NT, E])

        def per_expert(ap):
            return ap.unsqueeze(1).to_broadcast([P, NT, E])

        def route_top2(dve):
            def pick(src, top, onehot):
                then(dve, dve.tensor_reduce(top, src, AX, ALU.max))
                then(dve, dve.tensor_tensor(eq, src, per_token(top), ALU.is_equal))
                then(dve, dve.tensor_tensor(eq, eq, per_expert(sm["order"]), ALU.mult))
                then(dve, dve.tensor_reduce(sm["pm"], eq, AX, ALU.max))
                then(dve, dve.tensor_tensor(onehot, eq, per_token(sm["pm"]), ALU.is_equal))

            dve.wait_ge(s["tok0_read"], NT)
            dve.wait_ge(s["pt_ps"], NT)
            pick(scr, sm["m1"], oh1)
            then(dve, dve.scalar_tensor_tensor(out=rest, in0=oh1, scalar=-BIG, in1=scr, op0=ALU.mult, op1=ALU.add))
            pick(rest, sm["m2"], oh2)
            dve.tensor_tensor(both, oh1, oh2, ALU.add).then_inc(both_in, 1)
            dve.tensor_tensor(sm["dn"], sm["m2"], sm["m1"], ALU.subtract).then_inc(gate_exp, 1)

        def route_slots(dve):
            dve.wait_ge(s["att_ps"], NT)
            dve.memset(zeros, 0.0).then_inc(zeros_in, 1)
            dve.wait_ge(gate_exp, 2)
            then(dve, dve.tensor_scalar(sm["m1"], sm["ed"], 1.0, None, ALU.add))
            gate = sm["val"][:, :, :, 1]
            then(dve, dve.reciprocal(gate[:, :, 0], sm["m1"]))
            dve.tensor_tensor(gate[:, :, 1], sm["ed"], gate[:, :, 0], ALU.mult)
            dve.tensor_copy(sm["val"][:, :, :, 0], sm["tok"].unsqueeze(2).to_broadcast([P, NT, TOPK])).then_inc(val_in, 1)
            dve.wait_ge(counted, 1)
            then(dve, dve.tensor_copy(tot, bank[1][:, 0:TE].rearrange("p (t e) -> p e t", e=E)))
            for e in range(E):
                last = dve.tensor_tensor_scan(incl[:, e, :], sm["one"], tot[:, e, :], 0.0, ALU.mult, ALU.add)
            then(dve, last)
            then(dve, dve.tensor_tensor(excl, incl, tot, ALU.subtract))
            then(dve, dve.tensor_tensor(rank, bank[0][:, 0:TE].rearrange("p (t e) -> p t e", e=E),
                                   excl.rearrange("p e t -> p t e"), ALU.add))
            then(dve, dve.tensor_scalar(nbi, incl[:, :, NT - 1], float(G - 1), None, ALU.add))
            then(dve, dve.tensor_scalar(nbi, nbi, 8, None, ALU.arith_shift_right))
            then(dve, dve.tensor_copy(nbk, nbi))
            then(dve, dve.tensor_tensor_scan(incb, sm["one"][:, 0:E], nbk, 0.0, ALU.mult, ALU.add))
            then(dve, dve.tensor_tensor(offb, incb, nbk, ALU.subtract))
            then(dve, dve.tensor_scalar(offb, offb, float(G), None, ALU.mult))
            then(dve, dve.tensor_tensor(rank, rank, per_expert(offb), ALU.add))
            for c, onehot in enumerate((oh1, oh2)):
                then(dve, dve.tensor_tensor(prod, onehot, rank, ALU.mult))
                then(dve, dve.tensor_reduce(sm["rk"][:, :, c], prod, AX, ALU.add))
            then(dve, dve.tensor_copy(sm["ri"], sm["rk"]))
            then(dve, dve.tensor_scalar(sm["rp"], sm["ri"], P - 1, None, ALU.bitwise_and))
            then(dve, dve.tensor_copy(sm["pos"], sm["rp"].rearrange("p t c -> p (t c)")))
            then(dve, dve.tensor_scalar(sm["rp"], sm["ri"], 7, None, ALU.arith_shift_right))
            then(dve, dve.tensor_copy(sm["blk"], sm["rp"].rearrange("p t c -> p (t c)")))
            dve.wait_ge(s["stage_lo"], NT)

        def route_onehots(dve):
            with dve.Fori(0, NT * TOPK // CH // MB) as i:
                for m in range(MB):
                    cols = DS(i * (MB * CH) + m * CH, CH)
                    dve.wait_ge(hot_used, MB * i + m + 1)
                    dve.tensor_tensor(onehot_blk[m], blk_iota.unsqueeze(1).to_broadcast([P, CH, NB]),
                                      sm["blk"][:, cols].unsqueeze(2).to_broadcast([P, CH, NB]), ALU.is_equal)
                    dve.tensor_tensor(onehot_pos[m], pos_iota.unsqueeze(1).to_broadcast([P, CH, P]),
                                      sm["pos"][:, cols].unsqueeze(2).to_broadcast([P, CH, P]),
                                      ALU.is_equal).then_inc(hot_in, 1)
            dve.wait_ge(s["xnt"], NT)
            for b in range(B):
                dve.wait_ge(xn_stored[b], 16 * NW)
            then(dve, dve.tensor_tensor(cmp, incb.unsqueeze(1).to_broadcast([P, NG, E]),
                                   sm["jiota"].unsqueeze(2).to_broadcast([P, NG, E]), ALU.is_le))
            then(dve, dve.tensor_reduce(ta[:, 0:NG], cmp, AX, ALU.add))
            then(dve, dve.tensor_scalar(expert_of, ta[:, 0:NG], float(E - 1), None, ALU.min))
            dve.wait_ge(mapped, 1)
            table = bank[2][:, 0:2 * NB].rearrange("p (v n) -> p v n", v=2)
            dve.tensor_copy(slot_gate, table[:, 1, :])
            then(dve, dve.tensor_scalar(tb, table[:, 0, :], 0.0, sm["pcol"], ALU.is_equal, ALU.mult))
            then(dve, dve.scalar_tensor_tensor(out=slot_row, in0=table[:, 0, :], scalar=float(TOK), in1=tb,
                                          op0=ALU.add, op1=ALU.add))

        with nc.Block() as block:
            @block.sync
            def _(sp):
                def load_x(t, off):
                    sp.dma_start(xin[t.row(off)][:], x[DS(t.first_row(off), P), :]).then_inc(x_loaded[t.row(off)], 16)

                def load_weights(t, off):
                    m, w = t.row(off), (w1c, w2c)[t.row(off)]
                    sp.dma_start(stage[m][:], w[DS(t.window(off) * P, P), :]).then_inc(w_loaded[m], 16)

                def store_xn(t, off):
                    b = t.row(off)
                    t.wait(s["xn_in"], off)
                    sp.dma_start(xn_rows[DS(t.first_row(off), P), :], xn[b][:]).then_inc(xn_stored[b], 16)

                def step(t):
                    if t.has(-3):
                        b = t.row(-3)
                        t.wait(s["res_in"], -3)
                        sp.dma_start(out[DS(t.first_row(-3), P), :], res[b][:]).then_inc(res_stored[b], 16)
                    if t.has(-2):
                        b = t.row(-2)
                        t.wait(s["res_in"], -4)
                        sp.dma_start(xb[b][:], x[DS(t.first_row(-2), P), :]).then_inc(xb_loaded[b], 16)
                    if t.has(1):
                        store_xn(t, 1)
                    if t.has(3):
                        load_x(t, 3)
                    if t.has(2):
                        t.wait(s["stage_lo"], 0)
                        load_weights(t, 2)

                first = Step(sp, 0, 0)
                store_xn(first, 0)
                load_x(first, 2)
                steps(sp, step)
                for b in range(2):
                    sp.wait_ge(xn_stored[b], 16 * NW)
                    sp.wait_ge(res_stored[b], 16 * NW)

            @block.gpsimd
            def _(pool):
                wait_hi = tile_stepper(pool, "hi_value", 0)

                def step(t):
                    if t.has(-1):
                        b = t.row(-1)
                        t.wait(s["kexp_in"], -1)
                        pool.tensor_tensor(ke[b][:, 0:GD], ke[b][:, 0:GD], krelu[b][:], ALU.add).then_inc(s["ke_in"], 1)
                    if t.has(1):
                        rstd_of(t, 1)
                    if t.has(-2):
                        b = t.row(-2)
                        t.wait(s["new_in"], -2)
                        t.wait(s["att_ps"], -2)
                        pool.tensor_tensor(cum[b][:], cum0[b][:], new1[b][:], ALU.add).then_inc(s["cum_in"], 1)
                        if t.last(1):
                            route_constants(pool)
                        t.wait_dma(xb_loaded, -2)
                        pool.tensor_tensor(xb[b][:], xb[b][:], bias[:], ALU.add).then_inc(s["xb_in"], 1)
                    if t.has(0):
                        m = t.row(0)
                        hi, lo = ((w1h, w1l), (w2h, w2l))[m]
                        wait_hi(s["stage_hi"], t)
                        pool.tensor_scalar(stage[m][:], stage[m][:], WS, 1.0, ALU.mult, ALU.mult).then_inc(s["stage_up"], 1)
                        t.wait(s["stage_up"], 0)
                        pool.tensor_tensor(lo[:, DS(t.window(0) * F, F)], stage[m][:], hi[:, DS(t.window(0) * F, F)],
                                           ALU.subtract).then_inc(s["stage_lo"], 1)

                def rstd_of(t, off):
                    b = t.row(off)
                    t.wait(s["veps_in"], off)
                    pool.tensor_tensor(rstd[b][:], veps[b][:], minus_half[:], ALU.pow).then_inc(s["rstd_in"], 1)

                steps(pool, step)
                route_values(pool)

            @block.scalar
            def _(act):
                def step(t):
                    if t.has(0):
                        b = t.row(0)
                        t.wait(s["xnt"], 0)
                        t.wait(s["tok1"], -2)
                        act.activation(xth[b][:], b_xnt[:, 0:D], ACT.Copy, scale=XS).then_inc(s["xth_in"], 1)
                        hi = (w1h, w2h)[b]
                        t.wait_dma(w_loaded, 0)
                        act.activation(hi[:, DS(t.window(0) * F, F)], stage[b][:], ACT.Copy, scale=WS)\
                            .then_inc(s["stage_hi"], 1)
                    if t.has(-2):
                        b = t.row(-2)
                        t.wait(s["att_ps"], -2)
                        t.wait(s["at_ps"], -4)
                        act.activation(attn[b][:, LD:D], b_att[:, LD:D], ACT.Copy).then_inc(s["lin_in"], 1)
                    for half in range(2):
                        if t.has(-1):
                            b = t.row(-1)
                            t.wait(s[f"negmax{half}"], -1)
                            t.wait(s["rrec_in"], -3)
                            for h in range(2 * half, 2 * half + 2):
                                ins = act.activation(ss[:, h, :], ss[:, h, :], ACT.Exp, scale=-1.0,
                                                     bias=negmax[b][:, h:h + 1], accum_out=rsum[b][:, h:h + 1])
                            ins.then_inc(s[f"prob{half}"], 1)
                        if half == 0 and t.has(-2):
                            b = t.row(-2)
                            t.wait(s["at_ps"], -2)
                            t.wait(s["pr_ps"], -4)
                            act.activation(ath[b][:], b_out[:, 0:D], ACT.Copy, scale=AS).then_inc(s["ath_in"], 1)
                    if t.has(0):
                        b = t.row(0)
                        t.wait(s["qk"], 0)
                        t.wait(s["qt_in"], -2)
                        act.activation(qm[b][:], b_xnt[:, D:D + P], ACT.Copy,
                                       scale=low_row[:, LH:LH + 1]).then_inc(s["qm_in"], 1)
                        t.wait(s["head3"], -2)
                        act.activation(kt[b][:, 0, t.own(0)], b_xnt[:, D + P:D + 2 * P], ACT.Copy,
                                       scale=QS * UN_XW).then_inc(s["kh_in"], 1)
                        t.wait(s["qsub_in"], 0)
                        act.activation(qs[b][:, 0:GD], qs[b][:, 0:GD], ACT.Exp, scale=UN_XW).then_inc(s["qexp_in"], 1)
                    if t.has(-1):
                        t.wait(s["pt_ps"], -1)
                        t.wait(s["att_ps"], -2)
                        act.activation(pt[:, 2:4, :, :], b_s[1][:].rearrange("p (h c n) -> p h c n", h=2, c=2),
                                       ACT.Copy).then_inc(s["ptb_in"], 1)
                    if t.has(0):
                        b = t.row(0)
                        t.wait(s["ctx_ps"], -2)
                        act.activation(ke[b][:, 0:GD], b_tok0[:, CK:CK + GD], ACT.Relu, scale=-UN_XW)\
                            .then_inc(s["kneg_in"], 1)
                        t.wait(s["ke_in"], -2)
                        act.activation(krelu[b][:], b_tok0[:, CK:CK + GD], ACT.Relu, scale=UN_XW)
                        act.activation(scores[:, DS(b * NW + t.window(0), 1), :], b_tok0[:, CR:CR + E], ACT.Copy,
                                       scale=UN_XW).then_inc(s["tok0_read"], 1)
                        t.wait(s["kneg_in"], 0)
                        act.activation(ke[b][:, 0:GD], ke[b][:, 0:GD], ACT.Exp, scale=-1.0).then_inc(s["kexp_in"], 1)
                        t.wait(s["att_ps"], -2)
                        t.wait(s["tok1"], 0)
                        v = val[b][t.odd(0)]
                        act.activation(v[:, 0:LD + GA], b_tok1[:, 0:LD + GA], ACT.Copy, scale=UN_XW)
                        act.activation(v[:, LD + GA + 1:VC - 1], b_tok1[:, LD + GA:D], ACT.Copy,
                                       scale=UN_XW).then_inc(s["v_in"], 1)

                steps(act, step)
                route_act(act)

            @block.tensor
            def _(pe):
                def step(t):
                    if t.has(-3):
                        b = t.row(-3)
                        t.wait(s["atl_in"], -3)
                        at = (ath[b], atl[b])
                        three(pe, b_out[:, D:2 * D], lambda a, k: at[a][:, k * P:(k + 1) * P],
                              lambda c, k: wout[c][:, k, :], range(KC)).then_inc(s["pr_ps"], 1)
                    if t.has(0):
                        b = t.row(0)
                        t.wait(s["xn_in"], 0)
                        t.wait(s["kt_in"], -1)
                        for k in range(KC):
                            ins = pe.transpose(b_xnt[:, k * P:(k + 1) * P], xn[b][:, k * P:(k + 1) * P], ident[:])
                        ins.then_inc(s["xnt"], 1)
                    if t.has(-1):
                        t.wait(s["kt_in"], -1)
                    if t.has(-2):
                        t.wait(s["ptb_in"], -2)
                        t.wait(s["pta_in"], -2)
                    for h in range(LH):
                        if h % 2 and t.has(-1):
                            t.wait(s[f"head{h - 1}"], -1)
                        for a in range(2):
                            if t.has(-1):
                                b, c0, r = t.row(-1), (h % 2) * 2 * P, slice(32 * h, 32 * h + 32)
                                ins = pe.matmul(b_s[h // 2][:, c0:c0 + 2 * P], qt[b][r, :], kt[b][r, a, :],
                                                start=(a == 0), stop=(a == 1))
                                if a == 1:
                                    ins.then_inc(s[f"head{h}"], 1)
                            if t.has(-2):
                                b, c = t.row(-2), slice(h * DH, (h + 1) * DH)
                                pe.matmul(b_att[:, c], pt[:, h, a, :], val[b][a][:, c],
                                          start=(a == 0), stop=(a == 1))
                    if t.has(-2):
                        b = t.row(-2)
                        t.wait(s["qgt_in"], -2)
                        for u, state in enumerate((cum[b], cum0[b])):
                            r = slice(64 * u, 64 * u + 64)
                            pe.matmul(b_att[r, LD:LD + GA], qgt[b][:, 0, r], state[:, 0:GA], start=True, stop=True)
                            ins = pe.matmul(b_att[r, LD + GA:D], qgt[b][:, 1, r], state[:, GA + 1:GA + 1 + GB],
                                            start=True, stop=True)
                        ins.then_inc(s["att_ps"], 1)
                    if t.has(-1):
                        b = t.row(-1)
                        t.wait(s["qn_in"], -1)
                        t.wait(s["qgt_in"], -2)
                        for g in range(2):
                            ins = pe.transpose(b_ctx[:, g * P:(g + 1) * P], qs[b][:, g * P:(g + 1) * P], ident[:])
                        ins.then_inc(s["qgt_ps"], 1)
                        t.wait(s["ke_in"], -1)
                        t.wait(s["v_in"], -1)
                        v = val[b][t.odd(-1)]
                        for u, dst in ((0, b_ctx[:, D:D + CTX]), (1, b_tok1[:, D:D + CTX])):
                            r = slice(64 * u, 64 * u + 64)
                            pe.matmul(dst[:, 0:GA + 1], ke[b][r, 0:GA], v[r, LD:LD + GA + 1],
                                      start=True, stop=True)
                            ins = pe.matmul(dst[:, GA + 1:CTX], ke[b][r, GA:2 * GA], v[r, LD + GA + 1:VC],
                                            start=True, stop=True)
                        ins.then_inc(s["ctx_ps"], 1)
                    if t.has(-2):
                        b = t.row(-2)
                        t.wait(s["attn_in"], -2)
                        t.wait(s["res_in"], -3)
                        for k in range(KC):
                            ins = pe.transpose(b_out[:, k * P:(k + 1) * P], attn[b][:, k * P:(k + 1) * P], ident[:])
                        ins.then_inc(s["at_ps"], 1)
                    if t.has(0):
                        b = t.row(0)
                        t.wait(s["xtl_in"], 0)
                        t.wait(s["tok0_read"], -1)
                        xt = (xth[b], xtl[b])
                        lhs = lambda a, k: xt[a][:, k * P:(k + 1) * P]
                        three(pe, b_tok0[:, 0:CV], lhs, lambda c, k: wtok[c][:, k, 0:CV],
                              range(KC)).then_inc(s["tok0"], 1)
                        for m in range(2):
                            ins = three(pe, b_xnt[:, D + m * P:D + (m + 1) * P],
                                        lambda a, k: wqk[a][:, k, m, :, :, :].rearrange("p h c e -> p (h c e)"),
                                        lambda c, k: xt[c][:, k * P:(k + 1) * P], range(KC))
                        ins.then_inc(s["qk"], 1)
                    if t.has(-1):
                        for half in range(2):
                            t.wait(s[f"prob{half}"], -1)
                            for h in range(2 * half, 2 * half + 2):
                                for c in range(2):
                                    c0 = (h % 2) * 2 * P + c * P
                                    ins = pe.transpose(b_s[half][:, c0:c0 + P], ss[:, h, c * P:(c + 1) * P], ident[:])
                        ins.then_inc(s["pt_ps"], 1)
                    if t.has(0):
                        t.wait(s["v_in"], -1)
                        t.wait(s["new_in"], -1)
                        three(pe, b_tok1[:, 0:D], lhs, lambda c, k: wtok[c][:, k, CV:NTOKC],
                              range(KC)).then_inc(s["tok1"], 1)
                def step_or_route(t):
                    step(t)
                    if t.last(1):
                        route_counts(pe)

                steps(pe, step_or_route)
                route_tables(pe)

            @block.vector
            def _(dve):
                def spread(ap, n):
                    return ap.unsqueeze(len(ap.shape)).to_broadcast([*ap.shape, n])

                def heads(ap):
                    return ap.rearrange("p (h e) -> p h e", e=DH)

                wait_stats = tile_stepper(dve, "stats_value", 1)
                wait_scores = [tile_stepper(dve, f"scores{half}_value", -1) for half in range(2)]

                def mean_of(t, off):
                    b = t.row(off)
                    t.wait_dma(x_loaded, off)
                    dve.bn_stats(stats[b][:], xin[b][:]).then_inc(s["stats_in"], 1)

                def variance_of(t, off):
                    b = t.row(off)
                    wait_stats(s["stats_in"], t)
                    dve.bn_aggr(mv[b][:], stats[b][:]).then_inc(s["aggregated"], 1)
                    t.wait(s["aggregated"], off)
                    dve.tensor_scalar(veps[b][:], mv[b][:, 1:2], 1e-5, None, ALU.add).then_inc(s["veps_in"], 1)

                def normed(t, off):
                    b = t.row(off)
                    t.wait(s["rstd_in"], off)
                    t.wait(s["xnt"], off - 2)
                    t.wait_dma(xn_stored, off - 2)
                    dve.tensor_scalar(xn[b][:], xin[b][:], mv[b][:, 0:1], rstd[b][:], ALU.subtract,
                                      ALU.mult).then_inc(s["xn_in"], 1)

                def masked(t, half):
                    wait_scores[half](s[f"head{2 * half + 1}"], t)
                    mask = causal[:, 0:2 * P] if t.odd(-1) else causal[:, P:3 * P]
                    for h in (2 * half, 2 * half + 1):
                        c0 = (h % 2) * 2 * P
                        ins = dve.tensor_tensor_reduce(ss[:, h, :], b_s[half][:, c0:c0 + 2 * P], mask,
                                                       DH ** -0.5 / QS ** 2, BIG, ALU.add, ALU.min,
                                                       negmax[t.row(-1)][:, h:h + 1])
                    ins.then_inc(s[f"negmax{half}"], 1)

                def step(t):
                    if t.has(-3):
                        b = t.row(-3)
                        t.wait(s["pr_ps"], -3)
                        t.wait(s["xb_in"], -3)
                        t.wait_dma(res_stored, -5)
                        dve.scalar_tensor_tensor(out=res[b][:], in0=b_out[:, D:2 * D], scalar=UN_AW, in1=xb[b][:],
                                                 op0=ALU.mult, op1=ALU.add).then_inc(s["res_in"], 1)
                    if t.has(0):
                        b = t.row(0)
                        t.wait(s["xth_in"], 0)
                        dve.scalar_tensor_tensor(out=xtl[b][:], in0=b_xnt[:, 0:D], scalar=XS, in1=xth[b][:],
                                                 op0=ALU.mult, op1=ALU.subtract).then_inc(s["xtl_in"], 1)
                    if t.has(1):
                        mean_of(t, 1)
                    if t.has(1):
                        variance_of(t, 1)
                    if t.has(-1):
                        t.wait(s["pt_ps"], -2)
                        masked(t, 0)
                    if t.has(-2):
                        b = t.row(-2)
                        t.wait(s["prob1"], -2)
                        dve.reciprocal(rrec[b][:], rsum[b][:]).then_inc(s["rrec_in"], 1)
                    if t.has(-2):
                        b = t.row(-2)
                        t.wait(s["rrec_in"], -2)
                        t.wait(s["lin_in"], -2)
                        dve.tensor_tensor(heads(attn[b][:, 0:LD]), heads(b_att[:, 0:LD]), spread(rrec[b][:], DH),
                                          ALU.mult).then_inc(s["attn_in"], 1)
                    if t.has(-1):
                        b = t.row(-1)
                        masked(t, 1)
                        t.wait(s["ctx_ps"], -1)
                        t.wait(s["cum_in"], -3)
                        dve.tensor_tensor(new0[b][:], b_ctx[:, D:D + CTX], ctx_mask[:], ALU.mult).then_inc(s["new0_in"], 1)
                        dve.tensor_tensor(new1[b][:], b_tok1[:, D:D + CTX], ctx_mask[:], ALU.mult).then_inc(s["new_in"], 1)
                        dve.tensor_scalar(den[b][:, :, 0], cum[b][:, GA:CTX:GB + 1], 1e-6, None, ALU.add)
                        t.wait(s["new0_in"], -1)
                        dve.tensor_tensor(cum0[b][:], cum[b][:], new0[b][:], ALU.add).then_inc(s["cum0_in"], 1)
                    if t.has(-2):
                        b = t.row(-2)
                        t.wait(s["ath_in"], -2)
                        dve.scalar_tensor_tensor(out=atl[b][:], in0=b_out[:, 0:D], scalar=AS, in1=ath[b][:],
                                                 op0=ALU.mult, op1=ALU.subtract).then_inc(s["atl_in"], 1)
                    if t.has(-1):
                        b = t.row(-1)
                        t.wait(s["cum0_in"], -1)
                        dve.tensor_scalar(den[b][:, :, 1], cum0[b][:, GA:CTX:GB + 1], 1e-6, None,
                                          ALU.add).then_inc(s["den_in"], 1)
                    if t.has(1):
                        normed(t, 1)
                    if t.has(-1):
                        b = t.row(-1)
                        t.wait(s["den_in"], -1)
                        dve.reciprocal(rden[b][:], den[b][:]).then_inc(s["rden_in"], 1)
                    if t.has(0):
                        b = t.row(0)
                        t.wait(s["tok0"], 0)
                        dve.tensor_reduce(qmax[b][:], heads(b_tok0[:, CQ:CQ + GD]), AX, ALU.max).then_inc(s["qmax_in"], 1)
                    if t.has(-1):
                        b = t.row(-1)
                        t.wait(s["rden_in"], -1)
                        dve.tensor_tensor(qgt[b][:].rearrange("p g (u n) -> p g u n", u=2),
                                          b_ctx[:, 0:D].rearrange("p (g u n) -> p g u n", g=2, u=2),
                                          spread(rden[b][:], P // 2), ALU.mult).then_inc(s["qgt_in"], 1)
                    if t.has(0):
                        b = t.row(0)
                        t.wait(s["qmax_in"], 0)
                        t.wait(s["qgt_ps"], -2)
                        dve.tensor_tensor(heads(qs[b][:, 0:GD]), heads(b_tok0[:, CQ:CQ + GD]), spread(qmax[b][:], DH),
                                          ALU.subtract).then_inc(s["qsub_in"], 1)
                    if isinstance(t.i, int) and 2 * t.i + t.b == 2:
                        t.wait(s["negmax1"], -1)
                        dve.memset(causal[:, 2 * P:3 * P], 0.0).then_inc(opened, 1)
                        dve.wait_ge(opened, 1)
                    if t.has(0):
                        b = t.row(0)
                        t.wait(s["kh_in"], 0)
                        t.wait(s["head3"], -2)
                        dve.scalar_tensor_tensor(out=qt[b][:], in0=b_xnt[:, D:D + P], scalar=-QS * UN_XW, in1=qm[b][:],
                                                 op0=ALU.mult, op1=ALU.subtract).then_inc(s["qt_in"], 1)
                        dve.scalar_tensor_tensor(out=kt[b][:, 1, t.own(0)], in0=b_xnt[:, D + P:D + 2 * P],
                                                 scalar=QS * UN_XW, in1=kt[b][:, 0, t.own(0)],
                                                 op0=ALU.mult, op1=ALU.subtract).then_inc(s["kt_in"], 1)
                    if t.has(-1):
                        t.wait(s["pt_ps"], -1)
                        t.wait(s["att_ps"], -2)
                        dve.tensor_copy(pt[:, 0:2, :, :], b_s[0][:].rearrange("p (h c n) -> p h c n", h=2, c=2))\
                           .then_inc(s["pta_in"], 1)
                    if t.has(0):
                        b = t.row(0)
                        t.wait(s["qexp_in"], 0)
                        dve.tensor_reduce(qsum[b][:], heads(qs[b][:, 0:GD]), AX, ALU.add).then_inc(s["qsum_in"], 1)
                        t.wait(s["qsum_in"], 0)
                        dve.reciprocal(qrec[b][:], qsum[b][:]).then_inc(s["qrec_in"], 1)
                        t.wait(s["qrec_in"], 0)
                        dve.tensor_tensor(heads(qs[b][:, 0:GD]), heads(qs[b][:, 0:GD]), spread(qrec[b][:], DH),
                                          ALU.mult).then_inc(s["qn_in"], 1)

                def step_or_route(t):
                    step(t)
                    if t.last(0):
                        route_top2(dve)
                    if t.last(1):
                        route_slots(dve)

                steps(dve, step_or_route)
                route_onehots(dve)

        H = G // P
        FQ = FC // 4
        bX, bH, bY = bank[0], bank[1:5], bank[5:7]
        xg = [[xin[0], xin[1]], [xb[0], xb[1]]]
        yg = [[res[0], res[1]], [attn[0], attn[1]]]
        xh = [view(stage[0], m * D, KC, G, dt=F16) for m in range(2)]
        xl = [view(stage[0], (2 + m) * D, KC, G, dt=F16) for m in range(2)]
        hid = [view(buf, q * FQ * G, FQ * G) for buf in (ss, small) for q in range(2)]
        hh, hl = view(pt, 0, FC, G, dt=F16), view(spare[0], 0, FC, G, dt=F16)
        names = ("xgt xgh_in xgl_in h0 h1 h2 h3 hid0 hid1 hid2 hid3 hh0 hh1 hh2 hh3 hl0 hl1 hl2 hl3 "
                 "y_ps0 y_ps1 y_in0 y_in1 from_in to_in").split()
        e = {n: sem("e_" + n) for n in names}
        gathered = [sem(f"gathered{m}") for m in range(2)]
        scattered = [sem(f"scattered{m}") for m in range(2)]

        def groups(run, emit, first=0):
            for j in range(first):
                emit(j // 2, j % 2)
            with run.Fori(first // 2, (NG - 3) // 2) as i:
                for m in range(2):
                    emit(i, m)
            for j in range(NG - 3, NG):
                emit(j // 2, j % 2)

        def upto(i, m, ahead=0):
            return 2 * i + (m + ahead + 3)

        def slot(i, m, ahead):
            return (m + ahead) % 2, i + (m + ahead) // 2

        def beyond(i, m, ahead):
            return isinstance(i, int) and 2 * i + m + ahead >= NG

        def quarter(ap, q):
            return ap[:, q * FQ:(q + 1) * FQ, :].rearrange("p f n -> p (f n)")

        with nc.Block() as block:
            @block.gpsimd
            def _(pool):
                wait_rows = stepper(pool, "rows_value", 1)
                wait_y = [stepper(pool, f"y{h}_value", 3) for h in range(H)]

                def gather(i, m, ahead):
                    if beyond(i, m, ahead):
                        return
                    n, _k = slot(i, m, ahead)
                    pool.wait_ge(e["from_in"], upto(i, m, ahead))
                    wait_rows(e["xgt"])
                    for h in range(H):
                        pool.indirect_dma_start(out=xg[n][h][:], out_offset=None, in_=xn_rows,
                                                in_offset=bass.IndirectOffsetOnAxis(ap=rows_from[n][:, h:h + 1], axis=0))\
                            .then_inc(gathered[n], 16)

                def step(i, m):
                    gather(i, m, 3)
                    n, k = slot(i, m, -1)
                    pool.wait_ge(e["to_in"], upto(i, m))
                    for h in range(H):
                        if h:
                            pool.wait_ge(scattered[m], 16 * (H * i + h))
                        elif not (isinstance(k, int) and k < 0):
                            pool.wait_ge(scattered[n], 16 * (H * k + H))
                        wait_y[h](e[f"y_in{h}"])
                        pool.indirect_dma_start(out=out, in_=yg[m][h][:], in_offset=None, compute_op=ALU.add,
                                                out_offset=bass.IndirectOffsetOnAxis(ap=rows_to[m][:, h:h + 1], axis=0))\
                            .then_inc(scattered[m], 16)

                for n in range(3):
                    gather(0, n, 0)
                groups(pool, step, first=2)
                for m in range(2):
                    pool.wait_ge(scattered[m], 16 * H * ((NG + 1 - m) // 2))

            @block.tensor
            def _(pe):
                for n in ("xgt", "h0", "h1", "h2", "h3", "y_ps0", "y_ps1"):
                    pe.sem_inc(e[n], 2)

                def turn_rows(i, m, ahead):
                    if beyond(i, m, ahead):
                        return
                    n, k = slot(i, m, ahead)
                    pe.wait_ge(gathered[n], 16 * (H * k + H))
                    pe.wait_ge(e["xgl_in"], upto(i, m, ahead - 1))
                    for h in range(H):
                        for c in range(KC):
                            c0 = c * G + h * P
                            ins = pe.transpose(bX[:, c0:c0 + P], xg[n][h][:, c * P:(c + 1) * P], ident[:])
                    ins.then_inc(e["xgt"], 1)

                def first(i, m, ahead, between=lambda: None):
                    if beyond(i, m, ahead):
                        return
                    n, k = slot(i, m, ahead)
                    which = pe.value_load(expert_of[0:1, DS(2 * i + m + ahead, 1)], min_val=0, max_val=E - 1)
                    pe.wait_ge(e["xgl_in"], upto(i, m, ahead))
                    xt = (xh[n], xl[n])
                    for f in range(FC):
                        if f == FC // 2:
                            between()
                        if f % FQ == 0:
                            pe.wait_ge(e[f"hid{f // FQ}"], upto(i, m, ahead - 1))
                        ins = three(pe, bH[f // FQ][:, f % FQ * G:(f % FQ + 1) * G],
                                    lambda a, c: (w1h, w1l)[a][:, DS(which * (KC * F) + (c * F + f * P), P)],
                                    lambda a, c: xt[a][:, c, :], range(KC))
                        if f % FQ == FQ - 1:
                            ins.then_inc(e[f"h{f // FQ}"], 1)

                def step(i, m):
                    first(i, m, 1)
                    turn_rows(i, m, 2)
                    which = pe.value_load(expert_of[0:1, DS(2 * i + m, 1)], min_val=0, max_val=E - 1)
                    for h in range(H):
                        pe.wait_ge(e[f"y_in{h}"], upto(i, m, -1))
                        for f in range(FC):
                            if h == 0 and f % FQ == 0:
                                pe.wait_ge(e[f"hl{f // FQ}"], upto(i, m))
                            for a, c in ((0, 0), (0, 1), (1, 0)):
                                ins = pe.matmul(bY[h][:, 0:D], (hh, hl)[a][:, f, h * P:(h + 1) * P],
                                                (w2h, w2l)[c][:, DS(which * (FC * D) + f * D, D)],
                                                start=(f == a == c == 0), stop=(f == FC - 1 and a == 1))
                        ins.then_inc(e[f"y_ps{h}"], 1)

                turn_rows(0, 0, 0)
                first(0, 0, 0, between=lambda: turn_rows(0, 1, 0))
                groups(pe, step)

            @block.scalar
            def _(act):
                for n in ("xgh_in", "hid0", "hid1", "hid2", "hid3", "hh0", "hh1", "hh2", "hh3"):
                    act.sem_inc(e[n], 2)

                def rows_hi(i, m, ahead):
                    if beyond(i, m, ahead):
                        return
                    n, _k = slot(i, m, ahead)
                    act.wait_ge(e["xgt"], upto(i, m, ahead))
                    act.wait_ge(e["h3"], upto(i, m, ahead - 2))
                    act.activation(xh[n].rearrange("p k n -> p (k n)"), bX[:], ACT.Copy,
                                   scale=XS).then_inc(e["xgh_in"], 1)

                def gelu(i, m, ahead, between=lambda: None):
                    if beyond(i, m, ahead):
                        return
                    for q in range(4):
                        if q == 2:
                            between()
                        act.wait_ge(e[f"h{q}"], upto(i, m, ahead))
                        act.wait_ge(e[f"hl{q}"], upto(i, m, ahead - 1))
                        act.activation(hid[q], bH[q][:], ACT.Gelu, scale=UN_XW).then_inc(e[f"hid{q}"], 1)

                def step(i, m):
                    act.wait_ge(e["y_ps1"], upto(i, m, -1))
                    for q in range(4):
                        act.wait_ge(e[f"hid{q}"], upto(i, m))
                        act.activation(quarter(hh, q), hid[q], ACT.Copy, scale=HS).then_inc(e[f"hh{q}"], 1)
                    gelu(i, m, 1)
                    rows_hi(i, m, 2)

                rows_hi(0, 0, 0)
                gelu(0, 0, 0, between=lambda: rows_hi(0, 1, 0))
                groups(act, step)

            @block.vector
            def _(dve):
                for n in ("xgl_in", "hl0", "hl1", "hl2", "hl3", "y_in0", "y_in1", "from_in", "to_in"):
                    dve.sem_inc(e[n], 2)

                def rows_of(i, m, ahead):
                    if beyond(i, m, ahead):
                        return
                    n, k = slot(i, m, ahead)
                    if not (isinstance(k, int) and k == 0):
                        dve.wait_ge(gathered[n], 16 * H * k)
                    dve.tensor_copy(rows_from[n][:], slot_row[:, DS(4 * i + H * (m + ahead), H)]).then_inc(e["from_in"], 1)

                def rows_lo(i, m, ahead):
                    if beyond(i, m, ahead):
                        return
                    n, _k = slot(i, m, ahead)
                    dve.wait_ge(e["xgh_in"], upto(i, m, ahead))
                    dve.scalar_tensor_tensor(out=xl[n].rearrange("p k n -> p (k n)"), in0=bX[:], scalar=XS,
                                             in1=xh[n].rearrange("p k n -> p (k n)"),
                                             op0=ALU.mult, op1=ALU.subtract).then_inc(e["xgl_in"], 1)

                def step(i, m):
                    for q in range(4):
                        dve.wait_ge(e[f"hh{q}"], upto(i, m))
                        dve.scalar_tensor_tensor(out=quarter(hl, q), in0=hid[q], scalar=HS, in1=quarter(hh, q),
                                                 op0=ALU.mult, op1=ALU.subtract).then_inc(e[f"hl{q}"], 1)
                    rows_of(i, m, 3)
                    if not (isinstance(i, int) and i == 0):
                        dve.wait_ge(scattered[m], 16 * H * i)
                    dve.tensor_copy(rows_to[m][:], slot_row[:, DS(4 * i + H * m, H)]).then_inc(e["to_in"], 1)
                    rows_lo(i, m, 2)
                    for h in range(H):
                        dve.wait_ge(e[f"y_ps{h}"], upto(i, m))
                        dve.tensor_scalar(yg[m][h][:], bY[h][:, 0:D], slot_gate[:, DS(4 * i + (H * m + h), 1)], UN_HW,
                                          ALU.mult, ALU.mult).then_inc(e[f"y_in{h}"], 1)

                for n in range(3):
                    rows_of(0, n, 0)
                rows_lo(0, 0, 0)
                rows_lo(0, 1, 0)
                groups(dve, step, first=2)


def kernel(**inputs):
    import numpy as _np
    import concourse.bacc as _bacc
    from concourse import mybir as _mybir
    from concourse.bass_utils import run_bass_kernel_spmd as _run

    a = {n: _np.asarray(v) for n, v in inputs.items()}
    w1 = a["L0_ffn_expert_w1"].transpose(0, 2, 1)
    w2 = a["L0_ffn_expert_w2"].transpose(0, 2, 1)
    w2 = w2.reshape(E, 2, FC // 2, P, D).transpose(0, 1, 3, 2, 4)
    arrays = {
        "x": a["L0_attn_x"].reshape(TOK, D),
        "wq": a["L0_attn_Wq"], "wk": a["L0_attn_Wk"], "wv": a["L0_attn_Wv"], "wo": a["L0_attn_Wo"],
        "bo": a["L0_attn_bo"],
        "rwt": a["L0_ffn_router_w"].T,
        "w1c": w1.reshape(E * KC * P, F),
        "w2c": w2.reshape(E * 2 * P, FC // 2 * D),
    }
    arrays = {n: _np.ascontiguousarray(v) for n, v in arrays.items()}
    nc = _bacc.Bacc("TRN2", target_bir_lowering=False, num_devices=1)
    args = [nc.dram_tensor(n, v.shape, _mybir.dt.from_np(v.dtype), kind="ExternalInput").ap()
            for n, v in arrays.items()]
    out = nc.dram_tensor("out", (TOK + PAD, D), F32, kind="ExternalOutput").ap()
    block_kernel(nc, *args, out)
    got = _run(nc, [arrays], core_ids=[0]).results[0]["out"]
    return got[:TOK].reshape(B, SEQ, D)
```
